# Optimizing a Trainium2 kernel written in Bass

```python
import numpy as np
import jax
import jax.numpy as jnp

def _softmax(x, axis=-1):
    return jax.nn.softmax(x, axis=axis)

def _gelu(x):
    return jax.nn.gelu(x, approximate=True)

def _silu(x):
    return jax.nn.silu(x)

def _sigmoid(x):
    return jax.nn.sigmoid(x)

def _layernorm(x, axis=-1, eps=1e-05):
    m = jnp.mean(x, axis=axis, keepdims=True)
    v = jnp.var(x, axis=axis, keepdims=True)
    return (x - m) / jnp.sqrt(v + eps)

def _scatter_add(tgt, idx, src, axis=0):
    return tgt.at[idx].add(src)

def _segment_sum(src, seg, n):
    return jax.ops.segment_sum(src, seg, n)
kernel_name = 'mk_flamingo_gated_d2_seqx_r8_b63ef2'

def setup_inputs(seed: int=0):
    np.random.seed(seed)
    _w = jnp.asarray

    def _rec_inputs():
        import jax
        import jax.numpy as jnp
        _rk = jax.random.key(seed)
        x = -0.000125 + 0.9999 * jax.random.normal(jax.random.fold_in(_rk, 1), (8, 256, 256), jnp.float32)
        _lenS = 256 - jax.random.randint(jax.random.fold_in(_rk, 7), (8,), 0, max(1, 256 // 4) + 1, jnp.int32)
        _lenS2 = 64 - jax.random.randint(jax.random.fold_in(_rk, 8), (8,), 0, max(1, 64 // 4) + 1, jnp.int32)
        _ctx_2048P = jax.random.normal(jax.random.fold_in(_rk, 11), (8, 16, 256), jnp.float32)
        _ctx_2048c = jax.random.dirichlet(jax.random.fold_in(_rk, 511), 0.3 * jnp.ones((16,), jnp.float32), (8, 64))
        _ctx_2048t = jnp.einsum('bsk,bkd->bsd', _ctx_2048c, _ctx_2048P)
        _ctx_2048t = _ctx_2048t * jax.lax.rsqrt(jnp.mean(jnp.square(_ctx_2048t)) + 1e-12) * 0.953939
        ctx_2048 = -1.52775e-05 + 0.999936 * (_ctx_2048t + 0.3 * jax.random.normal(jax.random.fold_in(_rk, 611), (8, 64, 256), jnp.float32))
        _g = jax.random.normal(jax.random.fold_in(_rk, 9001), (2, 2), jnp.float32)
        _g = jnp.sign(_g) * jnp.maximum(jnp.abs(_g), 1.0) + (_g == 0) * 1.0
        g_xattn = _g[0]
        g_ffn = _g[1]
        return (x, ctx_2048, g_xattn, g_ffn)
    x, ctx_2048, g_xattn, g_ffn = _rec_inputs()

    def _L0_xattn_setup():
        import jax, jax.numpy as jnp
        import numpy as np
        EPS = 1e-06
        NUM_HEADS = 16

        def _feature_map(x):
            return jnp.where(x > 0, x + 1.0, jnp.exp(x))
        key = jax.random.key(seed)
        ks = jax.random.split(key, 7)
        B, L, S, D = (4, 512, 512, 256)
        sc = 1.0 / np.sqrt(D)
        return {'query': jax.random.normal(ks[0], (B, L, D), jnp.float32), 'kv': jax.random.normal(ks[1], (B, S, D), jnp.float32), 'Wq': jax.random.normal(ks[2], (D, D), jnp.float32) * sc, 'Wg': jax.random.normal(ks[3], (D, D), jnp.float32) * sc, 'bg': jnp.ones((D,), jnp.float32), 'Wkv': jax.random.normal(ks[4], (2 * D, D), jnp.float32) * sc, 'Wo': jax.random.normal(ks[5], (D, D), jnp.float32) * sc}
    _L0_xattn_all = _L0_xattn_setup()
    _L0_xattn_in = {k: v for k, v in _L0_xattn_all.items() if k in ('Wq', 'Wg', 'bg', 'Wkv', 'Wo')}
    del _L0_xattn_all

    def _L0_ffn_setup():
        import jax, jax.numpy as jnp
        import numpy as np
        E = 8
        TOP_K = 2
        H = 256
        I = 176
        SI = 704
        key = jax.random.key(seed)
        ks = jax.random.split(key, 9)
        s = lambda fan_in: 1.0 / np.sqrt(fan_in)
        return {'hidden_states': jax.random.normal(ks[0], (4, 256, H), dtype=jnp.float32), 'router_w': jax.random.normal(ks[1], (E, H), dtype=jnp.float32) * s(H), 'w_gate': jax.random.normal(ks[2], (E, H, I), dtype=jnp.float32) * s(H), 'w_up': jax.random.normal(ks[3], (E, H, I), dtype=jnp.float32) * s(H), 'w_down': jax.random.normal(ks[4], (E, I, H), dtype=jnp.float32) * s(I), 'sw_gate': jax.random.normal(ks[5], (H, SI), dtype=jnp.float32) * s(H), 'sw_up': jax.random.normal(ks[6], (H, SI), dtype=jnp.float32) * s(H), 'sw_down': jax.random.normal(ks[7], (SI, H), dtype=jnp.float32) * s(SI), 'shared_gate_w': jax.random.normal(ks[8], (H,), dtype=jnp.float32) * s(H)}
    _L0_ffn_all = _L0_ffn_setup()
    _L0_ffn_in = {k: v for k, v in _L0_ffn_all.items() if k in ('router_w', 'w_gate', 'w_up', 'w_down', 'sw_gate', 'sw_up', 'sw_down', 'shared_gate_w')}
    del _L0_ffn_all

    def _L1_xattn_setup():
        import jax, jax.numpy as jnp
        import numpy as np
        D_MODEL = 256
        NUM_HEADS = 16
        HEAD_DIM = D_MODEL // NUM_HEADS

        def _fq_sym(x, axis):
            s = jnp.max(jnp.abs(x), axis=axis, keepdims=True) / 127.0
            s = jnp.maximum(s, 1e-08)
            q = jnp.clip(jnp.round(x / s), -127.0, 127.0) * s
            return x + jax.lax.stop_gradient(q - x)

        def _fq_unsigned(x, axis):
            s = jnp.max(x, axis=axis, keepdims=True) / 255.0
            s = jnp.maximum(s, 1e-08)
            q = jnp.clip(jnp.round(x / s), 0.0, 255.0) * s
            return x + jax.lax.stop_gradient(q - x)
        key = jax.random.key(seed)
        ks = jax.random.split(key, 8)
        B, N, M, C = (2, 256, 64, D_MODEL)
        return {'x': jax.random.normal(ks[0], (B, N, C), jnp.float32), 'cond': jax.random.normal(ks[1], (B, M, C), jnp.float32), 'Wq': jax.random.normal(ks[2], (C, C), jnp.float32) * 0.02, 'bq': jnp.zeros((C,), jnp.float32), 'Wkv': jax.random.normal(ks[3], (C, 2 * C), jnp.float32) * 0.02, 'bkv': jnp.zeros((2 * C,), jnp.float32), 'Wp': jax.random.normal(ks[4], (C, C), jnp.float32) * 0.02, 'bp': jnp.zeros((C,), jnp.float32)}
    _L1_xattn_all = _L1_xattn_setup()
    _L1_xattn_in = {k: v for k, v in _L1_xattn_all.items() if k in ('Wq', 'bq', 'Wkv', 'bkv', 'Wp', 'bp')}
    del _L1_xattn_all

    def _L1_ffn_setup():
        import jax, jax.numpy as jnp
        import numpy as np
        B, S, H = (4, 256, 256)
        E, I, IS = (16, 176, 704)
        TOP_K = 4
        NORM_TOPK_PROB = False

        def _routing_weights(x, router_w):
            logits = x @ router_w.T
            probs = jax.nn.softmax(logits.astype(jnp.float32), axis=-1)
            vals, idx = jax.lax.top_k(probs, TOP_K)
            if NORM_TOPK_PROB:
                vals = vals / jnp.sum(vals, axis=-1, keepdims=True)
            T = x.shape[0]
            w_dense = jnp.zeros((T, probs.shape[-1]), probs.dtype)
            w_dense = w_dense.at[jnp.arange(T)[:, None], idx].set(vals)
            return w_dense.astype(x.dtype)

        def _moe_experts(x, gate_w, up_w, down_w, w_dense):

            def body(acc, ew):
                gw, uw, dw, w = ew
                h = jax.nn.silu(x @ gw.T) * (x @ uw.T)
                return (acc + w[:, None] * (h @ dw.T), None)
            acc, _ = jax.lax.scan(body, jnp.zeros_like(x), (gate_w, up_w, down_w, w_dense.T))
            return acc
        key = jax.random.key(seed)
        ks = jax.random.split(key, 9)
        s = 0.02
        return {'hidden_states': jax.random.normal(ks[0], (B, S, H), jnp.float32), 'router_w': jax.random.normal(ks[1], (E, H), jnp.float32) * s, 'gate_w': jax.random.normal(ks[2], (E, I, H), jnp.float32) * s, 'up_w': jax.random.normal(ks[3], (E, I, H), jnp.float32) * s, 'down_w': jax.random.normal(ks[4], (E, H, I), jnp.float32) * s, 'shared_gate_w': jax.random.normal(ks[5], (IS, H), jnp.float32) * s, 'shared_up_w': jax.random.normal(ks[6], (IS, H), jnp.float32) * s, 'shared_down_w': jax.random.normal(ks[7], (H, IS), jnp.float32) * s, 'se_gate_w': jax.random.normal(ks[8], (1, H), jnp.float32) * s}
    _L1_ffn_all = _L1_ffn_setup()
    _L1_ffn_in = {k: v for k, v in _L1_ffn_all.items() if k in ('router_w', 'gate_w', 'up_w', 'down_w', 'shared_gate_w', 'shared_up_w', 'shared_down_w', 'se_gate_w')}
    del _L1_ffn_all
    return {'x': x, 'ctx_2048': ctx_2048, 'g_xattn': g_xattn, 'g_ffn': g_ffn, 'L0_xattn_Wq': _L0_xattn_in['Wq'], 'L0_xattn_Wg': _L0_xattn_in['Wg'], 'L0_xattn_bg': _L0_xattn_in['bg'], 'L0_xattn_Wkv': _L0_xattn_in['Wkv'], 'L0_xattn_Wo': _L0_xattn_in['Wo'], 'L0_ffn_router_w': _L0_ffn_in['router_w'], 'L0_ffn_w_gate': _L0_ffn_in['w_gate'], 'L0_ffn_w_up': _L0_ffn_in['w_up'], 'L0_ffn_w_down': _L0_ffn_in['w_down'], 'L0_ffn_sw_gate': _L0_ffn_in['sw_gate'], 'L0_ffn_sw_up': _L0_ffn_in['sw_up'], 'L0_ffn_sw_down': _L0_ffn_in['sw_down'], 'L0_ffn_shared_gate_w': _L0_ffn_in['shared_gate_w'], 'L1_xattn_Wq': _L1_xattn_in['Wq'], 'L1_xattn_bq': _L1_xattn_in['bq'], 'L1_xattn_Wkv': _L1_xattn_in['Wkv'], 'L1_xattn_bkv': _L1_xattn_in['bkv'], 'L1_xattn_Wp': _L1_xattn_in['Wp'], 'L1_xattn_bp': _L1_xattn_in['bp'], 'L1_ffn_router_w': _L1_ffn_in['router_w'], 'L1_ffn_gate_w': _L1_ffn_in['gate_w'], 'L1_ffn_up_w': _L1_ffn_in['up_w'], 'L1_ffn_down_w': _L1_ffn_in['down_w'], 'L1_ffn_shared_gate_w': _L1_ffn_in['shared_gate_w'], 'L1_ffn_shared_up_w': _L1_ffn_in['shared_up_w'], 'L1_ffn_shared_down_w': _L1_ffn_in['shared_down_w'], 'L1_ffn_se_gate_w': _L1_ffn_in['se_gate_w']}

def reference(x, ctx_2048, g_xattn, g_ffn, L0_xattn_Wq, L0_xattn_Wg, L0_xattn_bg, L0_xattn_Wkv, L0_xattn_Wo, L0_ffn_router_w, L0_ffn_w_gate, L0_ffn_w_up, L0_ffn_w_down, L0_ffn_sw_gate, L0_ffn_sw_up, L0_ffn_sw_down, L0_ffn_shared_gate_w, L1_xattn_Wq, L1_xattn_bq, L1_xattn_Wkv, L1_xattn_bkv, L1_xattn_Wp, L1_xattn_bp, L1_ffn_router_w, L1_ffn_gate_w, L1_ffn_up_w, L1_ffn_down_w, L1_ffn_shared_gate_w, L1_ffn_shared_up_w, L1_ffn_shared_down_w, L1_ffn_se_gate_w):
    import jax
    import jax.numpy as jnp

    def _L0_xattn_ref(query, kv, Wq, Wg, bg, Wkv, Wo):
        import jax, jax.numpy as jnp
        import numpy as np
        EPS = 1e-06
        NUM_HEADS = 16

        def _feature_map(x):
            return jnp.where(x > 0, x + 1.0, jnp.exp(x))
        B, L, D = query.shape
        S = kv.shape[1]
        H = NUM_HEADS
        hd = D // H
        q = query @ Wq.T
        gate = jax.nn.sigmoid(query @ Wg.T + bg)
        kvp = kv @ Wkv.T
        k, v = jnp.split(kvp, 2, axis=-1)
        q = _feature_map(q.reshape(B, L, H, hd).transpose(0, 2, 1, 3))
        k = _feature_map(k.reshape(B, S, H, hd).transpose(0, 2, 1, 3))
        v = v.reshape(B, S, H, hd).transpose(0, 2, 1, 3)
        kv_summary = jnp.einsum('bhsd,bhse->bhde', k, v)
        k_sum = k.sum(axis=-2)
        z = 1.0 / (jnp.einsum('bhld,bhd->bhl', q, k_sum)[..., None] + EPS)
        attn = jnp.einsum('bhld,bhde->bhle', q, kv_summary) * z
        attn = attn.transpose(0, 2, 1, 3).reshape(B, L, D)
        out = attn * gate @ Wo.T
        return out

    def _L0_ffn_ref(hidden_states, router_w, w_gate, w_up, w_down, sw_gate, sw_up, sw_down, shared_gate_w):
        import jax, jax.numpy as jnp
        import numpy as np
        E = 8
        TOP_K = 2
        H = 256
        I = 176
        SI = 704
        B, S, Hd = hidden_states.shape
        x = hidden_states.reshape(-1, Hd)
        shared = jnp.einsum('ts,sh->th', jax.nn.silu(x @ sw_gate) * (x @ sw_up), sw_down)
        logits = x @ router_w.T
        probs = jax.nn.softmax(logits.astype(jnp.float32), axis=-1)
        top_w, top_i = jax.lax.top_k(probs, TOP_K)
        top_w = top_w / jnp.sum(top_w, axis=-1, keepdims=True)
        combine = jnp.sum(jax.nn.one_hot(top_i, E, dtype=x.dtype) * top_w[..., None].astype(x.dtype), axis=1)
        h = jax.nn.silu(jnp.einsum('th,ehi->eti', x, w_gate)) * jnp.einsum('th,ehi->eti', x, w_up)
        expert_out = jnp.einsum('eti,eih->eth', h, w_down)
        routed = jnp.einsum('eth,te->th', expert_out, combine)
        shared_out = jax.nn.sigmoid(x @ shared_gate_w)[:, None] * shared
        return (routed + shared_out).reshape(B, S, Hd)

    def _L1_xattn_ref(x, cond, Wq, bq, Wkv, bkv, Wp, bp):
        import jax, jax.numpy as jnp
        import numpy as np
        D_MODEL = 256
        NUM_HEADS = 16
        HEAD_DIM = D_MODEL // NUM_HEADS

        def _fq_sym(x, axis):
            s = jnp.max(jnp.abs(x), axis=axis, keepdims=True) / 127.0
            s = jnp.maximum(s, 1e-08)
            q = jnp.clip(jnp.round(x / s), -127.0, 127.0) * s
            return x + jax.lax.stop_gradient(q - x)

        def _fq_unsigned(x, axis):
            s = jnp.max(x, axis=axis, keepdims=True) / 255.0
            s = jnp.maximum(s, 1e-08)
            q = jnp.clip(jnp.round(x / s), 0.0, 255.0) * s
            return x + jax.lax.stop_gradient(q - x)
        B, N, C = x.shape
        H, hd = (NUM_HEADS, HEAD_DIM)
        q = (x @ Wq + bq).reshape(1, B * N, H, hd)
        kv = (cond @ Wkv + bkv).reshape(1, -1, 2, H, hd)
        k, v = (kv[:, :, 0], kv[:, :, 1])
        scale = 1.0 / np.sqrt(hd).astype(np.float32)
        q = jnp.transpose(q * scale, (0, 2, 1, 3))
        k = jnp.transpose(k, (0, 2, 1, 3))
        v = jnp.transpose(v, (0, 2, 1, 3))
        q = _fq_sym(q, axis=-1)
        k = _fq_sym(k, axis=-1)
        v = _fq_sym(v, axis=2)
        attn = jnp.einsum('bhqd,bhkd->bhqk', q, k)
        attn = jax.nn.softmax(attn.astype(jnp.float32), axis=-1)
        attn = _fq_unsigned(attn, axis=-1)
        out = jnp.einsum('bhqk,bhkd->bhqd', attn, v)
        out = jnp.transpose(out, (0, 2, 1, 3)).reshape(B, N, C)
        return out @ Wp + bp

    def _L1_ffn_ref(hidden_states, router_w, gate_w, up_w, down_w, shared_gate_w, shared_up_w, shared_down_w, se_gate_w):
        import jax, jax.numpy as jnp
        import numpy as np
        B, S, H = (4, 256, 256)
        E, I, IS = (16, 176, 704)
        TOP_K = 4
        NORM_TOPK_PROB = False

        def _routing_weights(x, router_w):
            logits = x @ router_w.T
            probs = jax.nn.softmax(logits.astype(jnp.float32), axis=-1)
            vals, idx = jax.lax.top_k(probs, TOP_K)
            if NORM_TOPK_PROB:
                vals = vals / jnp.sum(vals, axis=-1, keepdims=True)
            T = x.shape[0]
            w_dense = jnp.zeros((T, probs.shape[-1]), probs.dtype)
            w_dense = w_dense.at[jnp.arange(T)[:, None], idx].set(vals)
            return w_dense.astype(x.dtype)

        def _moe_experts(x, gate_w, up_w, down_w, w_dense):

            def body(acc, ew):
                gw, uw, dw, w = ew
                h = jax.nn.silu(x @ gw.T) * (x @ uw.T)
                return (acc + w[:, None] * (h @ dw.T), None)
            acc, _ = jax.lax.scan(body, jnp.zeros_like(x), (gate_w, up_w, down_w, w_dense.T))
            return acc
        b, s, h = hidden_states.shape
        x = hidden_states.reshape(-1, h)
        w_dense = _routing_weights(x, router_w)
        moe_out = _moe_experts(x, gate_w, up_w, down_w, w_dense)
        shared = jax.nn.silu(x @ shared_gate_w.T) * (x @ shared_up_w.T) @ shared_down_w.T
        shared = jax.nn.sigmoid(x @ se_gate_w.T) * shared
        return (moe_out + shared).reshape(b, s, h)
    x = x + jnp.tanh(g_xattn[0]) * _L0_xattn_ref(_layernorm(x, axis=-1), ctx_2048, L0_xattn_Wq, L0_xattn_Wg, L0_xattn_bg, L0_xattn_Wkv, L0_xattn_Wo)
    x = x + jnp.tanh(g_ffn[0]) * _L0_ffn_ref(_layernorm(x, axis=-1), L0_ffn_router_w, L0_ffn_w_gate, L0_ffn_w_up, L0_ffn_w_down, L0_ffn_sw_gate, L0_ffn_sw_up, L0_ffn_sw_down, L0_ffn_shared_gate_w)
    x = x + jnp.tanh(g_xattn[1]) * _L1_xattn_ref(_layernorm(x, axis=-1), ctx_2048, L1_xattn_Wq, L1_xattn_bq, L1_xattn_Wkv, L1_xattn_bkv, L1_xattn_Wp, L1_xattn_bp)
    x = x + jnp.tanh(g_ffn[1]) * _L1_ffn_ref(_layernorm(x, axis=-1), L1_ffn_router_w, L1_ffn_gate_w, L1_ffn_up_w, L1_ffn_down_w, L1_ffn_shared_gate_w, L1_ffn_shared_up_w, L1_ffn_shared_down_w, L1_ffn_se_gate_w)
    return x

_drawn_inputs = setup_inputs


def setup_inputs(seed=0):
    import zlib

    import numpy as np

    out = dict(_drawn_inputs(seed))
    spreads = {'g_ffn': (-1.0, 0.6),
     'L0_xattn_bg': (1.0, 0.2),
     'L1_xattn_bq': (0.0, 0.8),
     'L1_xattn_bkv': (0.0, 0.325),
     'L1_xattn_bp': (0.0, 0.1)}
    factors = {'L1_xattn_Wq': 8.0,
     'L1_xattn_Wkv': 4.153,
     'L1_ffn_router_w': 8.0,
     'L1_ffn_gate_w': 8.0,
     'L1_ffn_up_w': 8.0,
     'L1_ffn_down_w': 8.0,
     'L1_ffn_shared_gate_w': 5.384,
     'L1_ffn_shared_up_w': 5.347,
     'L1_ffn_shared_down_w': 5.335,
     'L1_ffn_se_gate_w': 8.0}
    for name, (base, spread) in spreads.items():
        noise = np.random.default_rng([zlib.crc32(name.encode()), seed]).standard_normal(out[name].shape)
        drawn = base * np.exp(spread * noise) if base else spread * noise
        out[name] = jnp.asarray(drawn.astype(out[name].dtype))
    for name, factor in factors.items():
        out[name] = (out[name] * factor).astype(out[name].dtype)
    return out
```

```python
from contextlib import ExitStack

import concourse.bass as bass
from concourse import mybir

F32 = mybir.dt.float32
F16 = mybir.dt.float16
I32 = mybir.dt.int32
U32 = mybir.dt.uint32
ACT = mybir.ActivationFunctionType
ALU = mybir.AluOpType
AX = mybir.AxisListType.X

P = 128
D = 256
C = D // P
HEADS, HD = 16, 16
MAGIC = 1.5 * 2.0 ** 23
SW = 256.0
LN255 = 5.541263545158426
LN_EPS = 1e-5
Z_EPS = 1e-6
HL = ((0, 0), (0, 1), (1, 0))


class Count:

    def __init__(self, sem, start):
        self.sem, self.start = sem, start


def gated_flamingo(nc, a, out, stage=99):
    T = a["x"].shape[0]
    NT = T // P
    CTX = a["ctxT"].shape[1]
    NB = 8
    TB = T // NB
    SB_ = CTX // NB
    KT = CTX // P
    EI = a["dn0"].shape[1]
    EG = 2 * EI
    EC = EI // 2
    SI = a["sdn0"].shape[0]
    SG = 2 * SI
    SCH = SG // P
    SFULL = SI // P
    SREM = SI - SFULL * P
    E = (a["gu0"].shape[0], a["gu1"].shape[0])
    TOPK = (2, 4)
    NS = tuple((T * TOPK[l] + E[l] * (P - 1)) // P for l in range(2))

    xs = [nc.dram_tensor(f"expert_in_{l}", [NS[l] * P, D], F32, kind="Internal").ap() for l in range(2)]
    ys = [nc.dram_tensor(f"expert_out_{l}", [NS[l] * P, D], F32, kind="Internal").ap() for l in range(2)]

    with ExitStack() as ctx:
        def sb(name, shape, dt=F32):
            return ctx.enter_context(nc.sbuf_tensor("sb_" + name, shape, dt))

        def sem(name):
            return ctx.enter_context(nc.semaphore(name))

        PS = ctx.enter_context(nc.psum_tensor("PS", [P, 8, 512], F32))

        x_sb = sb("x_sb", [P, NT, D])
        idf = sb("idf", [P, P])
        idh = sb("idh", [P, P], F16)
        ones_h = sb("ones_h", [P, P], F16)
        tri = sb("tri", [P, P], F16)
        headmask = sb("headmask", [P, P])
        lower = sb("lower", [P, 16, 16])
        tileno = sb("tileno", [1, max(NS)])
        swb = sb("swb", [P, 1])
        mhalf = sb("mhalf", [P, NT])
        zero = sb("zero", [P, D])

        wa0 = sb("wa0", [P, 2, C, 5 * D], F16)
        wa1 = sb("wa1", [P, 2, C, 4 * D], F16)
        rw = [sb(f"rw{l}", [P, 2, C, E[l] + 1], F16) for l in range(2)]
        ctxT = sb("ctxT_hl", [P, 2, C, CTX], F16)
        EXP_COLS = 16 * (2 * C * EG + 2 * 2 * D)
        region = sb("region", [P, EXP_COLS], F16)
        reg32 = region[:, :].bitcast(F32)
        half = EXP_COLS // 2
        GU = (region[:, half:half + 8 * 4 * EG // 1].rearrange("p (e h c n) -> p e h c n", e=8, h=2, c=C),
              region[:, 0:16 * 4 * EG].rearrange("p (e h c n) -> p e h c n", e=16, h=2, c=C))
        DN = (region[0:EC, half + 8 * 4 * EG:EXP_COLS].rearrange("p (e h c n) -> p e h c n", e=8, h=2, c=2),
              region[0:EC, 16 * 4 * EG:EXP_COLS].rearrange("p (e h c n) -> p e h c n", e=16, h=2, c=2))
        sgu = sb("sgu", [P, 2, C, SG], F16)
        sdn = sb("sdn", [P, 2, SFULL + 1, D], F16)
        stg = sb("stg", [P, 4, 2 * EG])

        xnT = sb("xnT", [P, 2, C, T], F16)
        KV = xnT[:, :, :, :].rearrange("p h c t -> p h (c t)").rearrange(
            "p h (b m k e) -> p h b m k e", b=NB, m=C, k=2)
        xnf = sb("xnf", [P, NT, D])
        Kpad = xnf[:, :, :].rearrange("p t d -> p (t d)").bitcast(F16).rearrange("p (h k) -> p h k", h=HEADS)
        Kg = Kpad.rearrange("p (g f) k -> p g f k", f=4)
        Vi = sb("Vi", [P, KT, D], F16)
        sv = sb("sv", [P, C])
        bq = sb("bq", [P, D])
        bk = sb("bk", [P, D])
        bp = sb("bp", [P, D])
        bv = sb("bv", [P, C])
        bg = sb("bg", [P, C])
        g4 = sb("g4", [P, 4])
        tg = sb("tg", [P, 4])
        tgw = sb("tgw", [P, 4])
        mv = sb("mv", [P, NT, 2])
        bst = sb("bst", [P, 6])
        mv1 = sb("mv1", [P, 2])
        ve = sb("ve", [P, NT])
        rstd = sb("rstd", [P, NT])
        wk1 = sb("wk1", [P, 4, 512])
        wkh = sb("wkh", [P, 8, 512], F16)
        w0_as_f32 = wa0[:, :, :, :].rearrange("p h c n -> p (h c n)").bitcast(F32)
        xg = w0_as_f32.rearrange("p (r d) -> p r d", d=D)
        xn32 = xnT[:, :, :, :].rearrange("p h c t -> p (h c t)").bitcast(F32)
        low32 = reg32[:, 6144:half // 2].rearrange("p (r n) -> p r n", n=512)
        lg = sb("lg", [P, NT, 17])
        ex = sb("ex", [P, NT, 16])
        rank = sb("rank", [P, NT, 16])
        selm = sb("selm", [P, NT + 1, 16], F16)
        slotv = sb("slotv", [P, NT, 16])
        sm = sb("sm", [P, 16, 16])
        slotk = sb("slotk", [P, 4, NT])
        slotu = sb("slotu", [P, 4, NT], U32)
        wsel = sb("wsel", [P, 4, NT])
        sgate = sb("sgate", [P, NT])
        texp = sb("texp", [1, max(NS)], I32)
        texpf = sb("texpf", [1, max(NS)])

        phase = sem("phase")
        const_ready = sem("const_ready")
        ld_x = sem("ld_x"); ld_ctx = sem("ld_ctx"); ld_w0 = sem("ld_w0"); ld_w1 = sem("ld_w1")
        ld_small = sem("ld_small"); ld_rw = sem("ld_rw")
        hi_done = sem("hi_done"); lo_done = sem("lo_done")
        tg_ready = sem("tg_ready"); tgw_ready = sem("tgw_ready")
        stg_loaded = [sem(f"stg_loaded{i}") for i in range(4)]
        stg_split = [sem(f"stg_split{i}") for i in range(4)]
        shared_ready = [sem(f"shared_ready{l}") for l in range(2)]
        experts_ready = [sem(f"experts_ready{l}") for l in range(2)]
        shared_used = sem("shared_used"); experts_used = sem("experts_used")
        zeroed = [sem(f"zeroed{l}") for l in range(2)]
        stats_ready = sem("stats_ready"); rstd_ready = sem("rstd_ready")
        out_done = sem("out_done")

        block = ctx.enter_context(nc.Block())

        def steps(eng, total, unroll, lead, tail, fn):
            rounds = (total - lead - tail) // unroll
            for s in range(lead):
                fn(0, s)
            with eng.Fori(0, rounds) as i:
                for s in range(unroll):
                    fn(i * unroll, lead + s)
            for s in range(lead + rounds * unroll, total):
                fn(0, s)

        def at_least(eng, s, base, n):
            if isinstance(base, int) and base + n <= 0:
                return
            assert isinstance(base, int) or n > 0, "a wait on a register's value has to be positive"
            if isinstance(s, Count):
                s, n = s.sem, n + s.start
            if isinstance(base, int):
                if base + n > 0:
                    eng.wait_ge(s, base + n)
            else:
                eng.wait_ge(s, base + n)

        def meet(eng, n):
            eng.drain().then_inc(phase, 1)
            eng.wait_ge(phase, 3 * n)

        w0f, w1f, ctxf = reg32[:, 0:2560], reg32[:, 2560:4608], reg32[:, 4608:5632]
        rwf = [reg32[:, 5632:5632 + C * 9], reg32[:, 5664:5664 + C * 17]]

        def inside(base, s, lo, hi):
            return not isinstance(base, int) or lo <= base + s < hi

        def bc(ap, n):
            return ap.unsqueeze(len(ap.shape)).broadcast_to(list(ap.shape) + [n])

        kv_ps = sem("kv_ps"); kv_parts = sem("kv_parts"); kv_k = sem("kv_k"); kv_kh = sem("kv_kh")
        kv_kl = sem("kv_kl"); sum_ps = sem("sum_ps"); sum_f = sem("sum_f"); sum_hi = sem("sum_hi")
        a_xn = sem("a_xn"); a_xT = sem("a_xT"); a_xh = sem("a_xh"); a_xl = sem("a_xl"); a_qg = sem("a_qg")
        a_act = sem("a_act"); a_phi = sem("a_phi"); a_phih = sem("a_phih"); a_phil = sem("a_phil")
        a_nd = sem("a_nd"); a_den = sem("a_den"); a_og = sem("a_og"); a_ogh = sem("a_ogh")
        a_ogl = sem("a_ogl"); a_out = sem("a_out"); a_x = sem("a_x")
        la_e, la_r, la_phi, la_den, la_og = (low32[:, i] for i in range(5))
        la_t = (low32[:, 5], low32[:, 6])
        la_xh, la_xl, la_ph, la_pl, la_oh, la_ol = (wkh[:, i] for i in range(6))

        z_eps = sb("z_eps", [P, 1])

        def stats(t):
            xt = x_sb[:, t, :] if isinstance(t, int) else x_sb[:, t, :].rearrange("p o d -> p (o d)")
            m = mv[:, t, :] if isinstance(t, int) else mv[:, t, :].rearrange("p o d -> p (o d)")
            nc.vector.bn_stats(bst[:, :], xt)
            nc.vector.drain()
            nc.vector.bn_aggr(mv1[:, :], bst[:, :])
            nc.vector.drain()
            nc.vector.tensor_copy(m, mv1[:, :])

        def stats_end(n):
            nc.vector.drain()
            nc.vector.tensor_scalar(ve[:, :], mv[:, :, 1], LN_EPS, None, ALU.add).then_inc(stats_ready, 1)

        def mm3(out_, lhs, rhs, more=False, begun=False):
            for c in range(C):
                for n, (i, j) in enumerate(HL):
                    last = nc.tensor.matmul(out_, lhs(i, c), rhs(j, c), start=(c == 0 and n == 0 and not begun),
                                            stop=(c == C - 1 and n == 2 and not more))
            return last

        KSH = SFULL + 1
        BLK = T // 512

        def both(name, *first):
            s = sem(name)
            return Count(s, 0), Count(s, first[0])

        r_xn = both("r_xn", NT)
        r_xT = both("r_xT", NT)
        r_xh = both("r_xh", NT)
        r_xl = both("r_xl", NT)
        r_lg = both("r_lg", NT)
        r_lgc = both("r_lgc", NT)
        r_shift = both("r_shift", 1)
        r_exp = both("r_exp", 1)
        r_sel = both("r_sel", 1)
        r_count = both("r_count", 1)
        r_slots = both("r_slots", 1)
        s_gu = both("s_gu", BLK * KSH)
        s_silu = both("s_silu", BLK * KSH)
        s_h = both("s_h", BLK * KSH)
        s_hh = both("s_hh", BLK * KSH)
        s_hl = both("s_hl", BLK * KSH)
        s_d = both("s_d", BLK * KSH)
        s_accr = both("s_accr", BLK)
        e_xT = both("e_xT", NS[0])
        e_xh = both("e_xh", NS[0])
        e_xl = both("e_xl", NS[0])
        e_gu = both("e_gu", NS[0])
        e_silu = both("e_silu", NS[0])
        e_h = both("e_h", NS[0])
        e_hT = both("e_hT", NS[0])
        e_hh = both("e_hh", NS[0])
        e_hl = both("e_hl", NS[0])
        e_d = both("e_d", NS[0])
        e_y = both("e_y", NS[0])
        e_ld = list(zip(*(both(f"e_ld{u}", 16 * ((NS[0] + 1 - u) // 2)) for u in range(2))))
        e_st = list(zip(*(both(f"e_st{u}", 16 * ((NS[0] + 1 - u) // 2)) for u in range(2))))
        c_ld = list(zip(*(both(f"c_ld{r}", 16 * len(range(r, NT * TOPK[0], 6))) for r in range(6))))
        c_used = both("c_used", NT * TOPK[0])
        scattered = both("scattered", 16 * NT * TOPK[0])

        def route_pe(pe, l):
            n = E[l] + 1
            for t in range(NT + 1):
                if t < NT:
                    at_least(pe, r_xn[l], 0, t + 1)
                    if t >= 2:
                        at_least(pe, r_xl[l], 0, t - 1)
                    for c in range(C):
                        last = nc.tensor.transpose(PS[:, t % 2, c * P:(c + 1) * P], xnf[:, t, c * P:(c + 1) * P], idf[:, :])
                    last.then_inc(r_xT[l].sem, 1)
                if t >= 1:
                    at_least(pe, r_xh[l], 0, t)
                    at_least(pe, r_xl[l], 0, t)
                    if t >= 3:
                        at_least(pe, r_lgc[l], 0, t - 2)
                    mm3(PS[:, 2 + (t - 1) % 2, 0:n], lambda i, c: xnT[:, i, c, (t - 1) * P:t * P],
                        lambda j, c: rw[l][:, j, c, :]).then_inc(r_lg[l].sem, 1)
            at_least(pe, r_sel[l], 0, 1)
            cnt = PS[:, 0, 0:(NT + 1) * E[l]]
            nc.tensor.matmul(cnt, tri[:, :], selm[:, :, 0:E[l]], start=True, stop=False, skip_group_check=True)
            for t in range(NT):
                last = nc.tensor.matmul(PS[:, 0, (t + 1) * E[l]:(NT + 1) * E[l]], ones_h[:, :],
                                        selm[:, t:t + 1, 0:E[l]].broadcast_to([P, NT - t, E[l]]),
                                        start=False, stop=(t == NT - 1), skip_group_check=True)
            last.then_inc(r_count[l].sem, 1)
            meet(pe, 3 + 5 * l)

        def route_act(act, l):
            for t in range(NT):
                at_least(act, r_xT[l], 0, t + 1)
                nc.scalar.activation(xnT[:, 0, :, t * P:(t + 1) * P],
                                     PS[:, t % 2, 0:D].rearrange("p (c n) -> p c n", c=C), ACT.Copy).then_inc(r_xh[l].sem, 1)
            at_least(act, r_shift[l], 0, 1)
            nc.scalar.activation(ex[:, :, 0:E[l]], ex[:, :, 0:E[l]], ACT.Exp)
            nc.scalar.activation(sm[:, 1, :], lg[:, :, E[l]], ACT.Exp, scale=-1.0).then_inc(r_exp[l].sem, 1)
            meet(act, 3 + 5 * l)

        def route_dve(dve, l):
            n, k_ = E[l], TOPK[l]
            dve.wait_ge(rstd_ready, 2 + 2 * l)
            for t in range(NT + 2):
                if t < NT:
                    nc.vector.tensor_scalar(xnf[:, t, :], x_sb[:, t, :], mv[:, t, 0:1], rstd[:, t:t + 1],
                                            ALU.subtract, ALU.mult).then_inc(r_xn[l].sem, 1)
                if 1 <= t <= NT:
                    at_least(dve, r_xh[l], 0, t)
                    s = slice((t - 1) * P, t * P)
                    nc.vector.tensor_tensor(xnT[:, 1, :, s], PS[:, (t - 1) % 2, 0:D].rearrange("p (c n) -> p c n", c=C),
                                            xnT[:, 0, :, s], ALU.subtract).then_inc(r_xl[l].sem, 1)
                if t >= 2:
                    at_least(dve, r_lg[l], 0, t - 1)
                    nc.vector.tensor_scalar(lg[:, t - 2, 0:n + 1], PS[:, 2 + t % 2, 0:n + 1], 1 / SW, None,
                                            ALU.mult).then_inc(r_lgc[l].sem, 1)
            dve.drain()
            L = lg[:, :, 0:n]
            nc.vector.tensor_reduce(sm[:, 0, :], L, AX, ALU.max)
            dve.drain()
            nc.vector.tensor_tensor(ex[:, :, 0:n], L, bc(sm[:, 0, :], n), ALU.subtract).then_inc(r_shift[l].sem, 1)
            for t in range(0, NT, 4):
                gt = wk1[:, 0:2].rearrange("p a b -> p (a b)")[:, 0:4 * n * n].rearrange("p (t e f) -> p t e f", t=4, e=n)
                eq = wk1[:, 2:4].rearrange("p a b -> p (a b)")[:, 0:4 * n * n].rearrange("p (t e f) -> p t e f", t=4, e=n)
                f_ = lg[:, t:t + 4, 0:n].unsqueeze(2).broadcast_to([P, 4, n, n])
                e_ = lg[:, t:t + 4, 0:n].unsqueeze(3).broadcast_to([P, 4, n, n])
                dve.drain()
                nc.vector.tensor_tensor(gt, f_, e_, ALU.is_gt)
                nc.vector.tensor_tensor(eq, f_, e_, ALU.is_equal)
                dve.drain()
                nc.vector.tensor_tensor(eq, eq, lower[:, 0:n, 0:n].unsqueeze(1).broadcast_to([P, 4, n, n]), ALU.mult)
                dve.drain()
                nc.vector.tensor_tensor(gt, gt, eq, ALU.add)
                dve.drain()
                nc.vector.tensor_reduce(rank[:, t:t + 4, 0:n], gt, AX, ALU.add)
            dve.drain()
            R = rank[:, :, 0:n]
            nc.vector.tensor_scalar(selm[:, 0:NT, 0:n], R, float(k_), None, ALU.is_lt).then_inc(r_sel[l].sem, 1)
            at_least(dve, r_exp[l], 0, 1)
            hot = wk1[:, 0:2].rearrange("p a b -> p (a b)")[:, 0:NT * n].rearrange("p (t e) -> p t e", e=n)
            for k in range(k_):
                nc.vector.scalar_tensor_tensor(hot, R, float(k), ex[:, :, 0:n], ALU.is_equal, ALU.mult)
                dve.drain()
                nc.vector.tensor_reduce(wsel[:, k, :], hot, AX, ALU.add)
                dve.drain()
            if l == 0:
                nc.vector.tensor_tensor(sm[:, 2, :], wsel[:, 0, :], wsel[:, 1, :], ALU.add)
            else:
                nc.vector.tensor_reduce(sm[:, 2, :], ex[:, :, 0:n], AX, ALU.add)
            nc.vector.tensor_scalar(sm[:, 1, :], sm[:, 1, :], 1.0, None, ALU.add)
            dve.drain()
            nc.vector.reciprocal(sm[:, 2, :], sm[:, 2, :])
            nc.vector.reciprocal(sm[:, 1, :], sm[:, 1, :])
            dve.drain()
            for k in range(k_):
                nc.vector.scalar_tensor_tensor(wsel[:, k, :], wsel[:, k, :], tgw[:, 2 + l:3 + l], sm[:, 2, :],
                                               ALU.mult, ALU.mult)
            nc.vector.tensor_scalar(sgate[:, :], sm[:, 1, :], tgw[:, 2 + l:3 + l], None, ALU.mult)
            at_least(dve, r_count[l], 0, 1)
            nc.vector.tensor_scalar(sm[:, 3, 0:n], PS[:, 0, NT * n:(NT + 1) * n], 1 / P,
                                    (P - 1) / P - 0.5 + 0.5 / P, ALU.mult, ALU.add)
            dve.drain()
            nc.vector.tensor_scalar(sm[:, 3, 0:n], sm[:, 3, 0:n], MAGIC, -MAGIC, ALU.add, ALU.add)
            dve.drain()
            pre = wk1[:, 2, 0:n * n].rearrange("p (e f) -> p e f", e=n)
            nc.vector.tensor_tensor(pre, sm[:, 3:4, 0:n].broadcast_to([P, n, n]), lower[:, 0:n, 0:n], ALU.mult)
            dve.drain()
            nc.vector.tensor_reduce(sm[:, 4, 0:n], pre, AX, ALU.add)
            dve.drain()
            nc.vector.tensor_tensor(sm[:, 5, 0:n], sm[:, 4, 0:n], sm[:, 3, 0:n], ALU.add)
            nc.vector.tensor_scalar(sm[:, 6, 0:n], sm[:, 4, 0:n], float(P), None, ALU.mult)
            dve.drain()
            nc.vector.tensor_tensor(slotv[:, :, 0:n], PS[:, 0, 0:NT * n].rearrange("p (t e) -> p t e", e=n),
                                    sm[:, 6:7, 0:n].broadcast_to([P, NT, n]), ALU.add)
            dve.drain()
            for k in range(k_):
                nc.vector.scalar_tensor_tensor(hot, R, float(k), slotv[:, :, 0:n], ALU.is_equal, ALU.mult)
                dve.drain()
                nc.vector.tensor_reduce(slotk[:, k, :], hot, AX, ALU.add)
                dve.drain()
            nc.vector.tensor_copy(slotu[:, 0:k_, :], slotk[:, 0:k_, :])
            w = wk1[:, :, :].rearrange("p a b -> p (a b)")[0:1, 0:NS[l] * n].rearrange("p (j e) -> p j e", e=n)
            nc.vector.tensor_tensor(w, bc(tileno[:, 0:NS[l]], n), sm[0:1, 5:6, 0:n].broadcast_to([1, NS[l], n]), ALU.is_ge)
            dve.drain()
            nc.vector.tensor_reduce(texpf[:, 0:NS[l]], w, AX, ALU.add)
            dve.drain()
            nc.vector.tensor_scalar(texp[:, 0:NS[l]], texpf[:, 0:NS[l]], float(n - 1), None, ALU.min)
            dve.drain().then_inc(r_slots[l].sem, 1)
            meet(dve, 3 + 5 * l)

        def tile_rows(ap, base, s):
            v = ap.rearrange("(t p) d -> t p d", p=P)
            return v[base + s] if isinstance(base, int) else \
                v[bass.ds(base + s, 1), :, :].rearrange("o p d -> (o p) d")

        def ffn_dma(sp, l):
            at_least(sp, scattered[l], 0, 16 * NT * TOPK[l])

            def slot_tile(base, s):
                u = s % 2
                if inside(base, s, 0, NS[l]):
                    at_least(sp, e_xT[l], base, s - 1)
                    sp.dma_start(xg[:, u, :], tile_rows(xs[l], base, s)).then_inc(e_ld[l][u].sem, 16)
                if inside(base, s, 2, NS[l] + 2):
                    at_least(sp, e_y[l], base, s - 1)
                    sp.dma_start(tile_rows(ys[l], base, s - 2), xg[:, 2 + u, :]).then_inc(e_st[l][u].sem, 16)
            steps(sp, NS[l] + 2, 2, 2, 2, slot_tile)

        def ffn_pool(pl, l):
            at_least(pl, r_slots[l], 0, 1)
            pl.wait_ge(zeroed[l], 16)
            for t in range(NT):
                for k in range(TOPK[l]):
                    nc.gpsimd.indirect_dma_start(xs[l][:, :], bass.IndirectOffsetOnAxis(ap=slotu[:, k, t:t + 1], axis=0),
                                                 xnf[:, t, :], None).then_inc(scattered[l].sem, 16)
            for u in range(2):
                at_least(pl, e_st[l][u], 0, 16 * ((NS[l] + 1 - u) // 2))
            for n in range(NT * TOPK[l]):
                t, k, r = n // TOPK[l], n % TOPK[l], n % 6
                if n >= 6:
                    at_least(pl, c_used[l], 0, n - 5)
                nc.gpsimd.indirect_dma_start(xg[:, 4 + r, :], None, ys[l][:, :],
                                             bass.IndirectOffsetOnAxis(ap=slotu[:, k, t:t + 1], axis=0))\
                    .then_inc(c_ld[l][r].sem, 16)

        def ffn_pe(pe, l):
            pe.wait_ge(shared_ready[l], 1)

            def shared_step(base, s):
                u, k, b = s % 2, s % KSH, s // KSH
                q6 = base * KSH
                if inside(base, b, 0, BLK):
                    at_least(pe, s_h[l], q6, s - 1)
                    lo_ = (base + b) * 512 if isinstance(base, int) else None
                    rhs = (lambda j, c: xnT[:, j, c, lo_:lo_ + 512]) if lo_ is not None else \
                        (lambda j, c: xnT[:, j, c, bass.ds(base * 512 + b * 512, 512)])
                    for h in range(2 if k < SFULL else 1):
                        last = mm3(PS[:, 2 * u + h, :], lambda i, c: sgu[:, i, c, (2 * k + h) * P:(2 * k + h + 1) * P], rhs)
                    last.then_inc(s_gu[l].sem, 1)
                if inside(base, s, 1, 10 ** 6):
                    kd, v = (s - 1) % KSH, (s - 1) % 2
                    r = P if kd < SFULL else SREM
                    at_least(pe, s_hh[l], q6, s)
                    at_least(pe, s_hl[l], q6, s)
                    if kd == 0:
                        at_least(pe, s_accr[l], base, (s - 1) // KSH)
                    for i in range(4):
                        for n, (h, j) in enumerate(HL):
                            last = nc.tensor.matmul(PS[:, 4 + i, 0:D], wkh[0:r, 2 * h + v, i * P:(i + 1) * P],
                                                    sdn[0:r, j, kd, :], start=(kd == 0 and n == 0),
                                                    stop=(kd == KSH - 1 and n == 2))
                    last.then_inc(s_d[l].sem, 1)
            blocks(pe, shared_step)
            pe.drain().then_inc(shared_used, 1)
            meet(pe, 4 + 5 * l)

            pe.wait_ge(experts_ready[l], 1)
            at_least(pe, r_slots[l], 0, 1)

            def transposes(base, s):
                at_least(pe, e_ld[l][s % 2], base * 8, 16 * (s // 2 + 1))
                at_least(pe, e_xl[l], base, s - 1)
                for c in range(C):
                    last = nc.tensor.transpose(PS[:, s % 2, c * P:(c + 1) * P], xg[:, s % 2, c * P:(c + 1) * P], idf[:, :])
                last.then_inc(e_xT[l].sem, 1)

            def expert(base, s):
                j = slice(base + s, base + s + 1) if isinstance(base, int) else bass.ds(base + s, 1)
                return pe.value_load(texp[0:1, j], min_val=0, max_val=E[l] - 1)

            def slot_tile(base, s):
                u = s % 2
                if inside(base, s, 0, NS[l]):
                    e = expert(base, s)
                    at_least(pe, e_xh[l], base, s + 1)
                    at_least(pe, e_xl[l], base, s + 1)
                    at_least(pe, e_h[l], base, s - 1)
                    mm3(PS[:, 2 + u, 0:EG], lambda i, c: wkh[:, u, i * D + c * P:i * D + (c + 1) * P],
                        lambda h, c: GU[l][:, bass.ds(e, 1), h, c, :].rearrange("p o n -> p (o n)")).then_inc(e_gu[l].sem, 1)
                    if inside(base, s, 0, NS[l] - 1):
                        transposes(base, s + 1)
                if inside(base, s, 1, NS[l] + 1):
                    v = (s - 1) % 2
                    e = expert(base, s - 1)
                    at_least(pe, e_hh[l], base, s)
                    at_least(pe, e_hl[l], base, s)
                    at_least(pe, e_y[l], base, s - 2)
                    mm3(PS[:, 6 + v, 0:D], lambda i, c: wkh[0:EC, 2 + v, i * D + c * P:i * D + (c + 1) * P],
                        lambda h, c: DN[l][:, bass.ds(e, 1), h, c, :].rearrange("p o n -> p (o n)")).then_inc(e_d[l].sem, 1)
                if inside(base, s, 0, NS[l]):
                    at_least(pe, e_h[l], base, s + 1)
                    at_least(pe, e_hl[l], base, s - 1)
                    for c in range(C):
                        last = nc.tensor.transpose(PS[0:EC, 4 + u, c * P:(c + 1) * P],
                                                   wk1[:, 2 + u, c * EC:(c + 1) * EC], idf[:, :])
                    last.then_inc(e_hT[l].sem, 1)
            transposes(0, 0)
            steps(pe, NS[l] + 1, 2, 3, 2, slot_tile)
            pe.drain().then_inc(experts_used, 1)
            meet(pe, 5 + 5 * l)

        def blocks(eng, fn):
            fn(0, 0)
            fn(0, 1)
            with eng.Fori(0, BLK - 1) as i:
                for s in range(2, KSH + 2):
                    fn(i, s)
            for s in range(2, KSH + 1):
                fn(BLK - 1, s)

        def ffn_act(act, l):
            def shared_step(base, s):
                u, k, b = s % 2, s % KSH, s // KSH
                q6 = base * KSH
                if inside(base, b, 0, BLK):
                    r = P if k < SFULL else SREM
                    at_least(act, s_gu[l], q6, s + 1)
                    at_least(act, s_h[l], q6, s - 1)
                    nc.scalar.activation(wk1[0:r, u, :], PS[0:r, 2 * u, :], ACT.Silu, scale=1 / SW).then_inc(s_silu[l].sem, 1)
                    at_least(act, s_h[l], q6, s + 1)
                    at_least(act, s_d[l], q6, s - 1)
                    nc.scalar.activation(wkh[0:r, u, :], wk1[0:r, 2 + u, :], ACT.Copy).then_inc(s_hh[l].sem, 1)
            blocks(act, shared_step)
            meet(act, 4 + 5 * l)

            def high_x(base, s):
                at_least(act, e_xT[l], base, s + 1)
                at_least(act, e_gu[l], base, s - 1)
                nc.scalar.activation(wkh[:, s % 2, 0:D], PS[:, s % 2, 0:D], ACT.Copy).then_inc(e_xh[l].sem, 1)

            def slot_tile(base, s):
                u = s % 2
                at_least(act, e_gu[l], base, s + 1)
                at_least(act, e_h[l], base, s - 1)
                nc.scalar.activation(wk1[:, u, 0:EI], PS[:, 2 + u, 0:EI], ACT.Silu, scale=1 / SW).then_inc(e_silu[l].sem, 1)
                if inside(base, s, 0, NS[l] - 1):
                    high_x(base, s + 1)
                at_least(act, e_hT[l], base, s + 1)
                at_least(act, e_d[l], base, s - 1)
                nc.scalar.activation(wkh[0:EC, 2 + u, 0:D], PS[0:EC, 4 + u, 0:D], ACT.Copy).then_inc(e_hh[l].sem, 1)
            high_x(0, 0)
            steps(act, NS[l], 2, 2, 1, slot_tile)
            meet(act, 5 + 5 * l)

        def ffn_dve(dve, l):
            def shared_out(base, b):
                at_least(dve, s_d[l], base * KSH, (b + 1) * KSH)
                for i in range(4):
                    if isinstance(base, int):
                        t = 4 * (base + b) + i
                        xt, g = x_sb[:, t, :], sgate[:, t:t + 1]
                    else:
                        t = bass.ds(base * 4 + (4 * b + i), 1)
                        xt, g = x_sb[:, t, :].rearrange("p o d -> p (o d)"), sgate[:, t]
                    last = nc.vector.scalar_tensor_tensor(xt, PS[:, 4 + i, 0:D], g, xt, ALU.mult, ALU.add)
                last.then_inc(s_accr[l].sem, 1)

            def shared_step(base, s):
                u, k, b = s % 2, s % KSH, s // KSH
                q6 = base * KSH
                if k == 1 and inside(base, b, 1, 10 ** 6) and s > KSH:
                    shared_out(base, b - 1)
                if inside(base, b, 0, BLK):
                    r = P if k < SFULL else SREM
                    at_least(dve, s_silu[l], q6, s + 1)
                    at_least(dve, s_hh[l], q6, s - 1)
                    up = PS[0:r, 2 * u + 1, :] if k < SFULL else PS[SREM:2 * SREM, 2 * u, :]
                    nc.vector.scalar_tensor_tensor(wk1[0:r, 2 + u, :], up, 1 / SW, wk1[0:r, u, :],
                                                   ALU.mult, ALU.mult).then_inc(s_h[l].sem, 1)
                    at_least(dve, s_hh[l], q6, s + 1)
                    at_least(dve, s_d[l], q6, s - 1)
                    nc.vector.tensor_tensor(wkh[0:r, 2 + u, :], wk1[0:r, 2 + u, :], wkh[0:r, u, :],
                                            ALU.subtract).then_inc(s_hl[l].sem, 1)
            blocks(dve, shared_step)
            shared_out(BLK - 1, 0)
            meet(dve, 4 + 5 * l)

            def low_x(base, s):
                at_least(dve, e_xh[l], base, s + 1)
                at_least(dve, e_gu[l], base, s - 1)
                nc.vector.tensor_tensor(wkh[:, s % 2, D:2 * D], PS[:, s % 2, 0:D], wkh[:, s % 2, 0:D],
                                        ALU.subtract).then_inc(e_xl[l].sem, 1)

            def slot_tile(base, s):
                u = s % 2
                if inside(base, s, 0, NS[l]):
                    at_least(dve, e_silu[l], base, s + 1)
                    at_least(dve, e_hT[l], base, s - 1)
                    nc.vector.scalar_tensor_tensor(wk1[:, 2 + u, 0:EI], PS[:, 2 + u, EI:EG], 1 / SW, wk1[:, u, 0:EI],
                                                   ALU.mult, ALU.mult).then_inc(e_h[l].sem, 1)
                    if inside(base, s, 0, NS[l] - 1):
                        low_x(base, s + 1)
                if inside(base, s, 1, NS[l] + 1):
                    v = (s - 1) % 2
                    at_least(dve, e_d[l], base, s)
                    at_least(dve, e_st[l][v], base * 8, 16 * ((s - 1) // 2))
                    nc.vector.tensor_copy(xg[:, 2 + v, :], PS[:, 6 + v, 0:D]).then_inc(e_y[l].sem, 1)
                if inside(base, s, 0, NS[l]):
                    at_least(dve, e_hh[l], base, s + 1)
                    at_least(dve, e_d[l], base, s - 1)
                    nc.vector.tensor_tensor(wkh[0:EC, 2 + u, D:2 * D], PS[0:EC, 4 + u, 0:D], wkh[0:EC, 2 + u, 0:D],
                                            ALU.subtract).then_inc(e_hl[l].sem, 1)
            low_x(0, 0)
            steps(dve, NS[l] + 1, 2, 3, 2, slot_tile)
            for n in range(NT * TOPK[l]):
                t, k, r = n // TOPK[l], n % TOPK[l], n % 6
                at_least(dve, c_ld[l][r], 0, 16 * (n // 6 + 1))
                dve.drain()
                nc.vector.scalar_tensor_tensor(x_sb[:, t, :], xg[:, 4 + r, :], wsel[:, k, t:t + 1], x_sb[:, t, :],
                                               ALU.mult, ALU.add).then_inc(c_used[l].sem, 1)
                if k == TOPK[l] - 1 and l == 0:
                    dve.drain()
                    stats(t)
            if l == 0:
                stats_end(2)
            meet(dve, 5 + 5 * l)

        p_v = sem("p_v"); p_vq = sem("p_vq"); p_vT = sem("p_vT"); p_vd = sem("p_vd"); p_k = sem("p_k")
        p_kq = sem("p_kq"); p_kT = sem("p_kT"); p_kd = sem("p_kd"); p_zero = sem("p_zero")
        q_xn = sem("q_xn"); q_xT = sem("q_xT"); q_xh = sem("q_xh"); q_xl = sem("q_xl"); q_ps = sem("q_ps")
        q_int = sem("q_int"); q_T = sem("q_T"); q_ready = sem("q_ready")
        h_qk = sem("h_qk"); h_max = sem("h_max"); h_exp = sem("h_exp"); h_int = sem("h_int"); h_pT = sem("h_pT")
        h_pc = sem("h_pc"); h_pv = sem("h_pv")
        o_norm = sem("o_norm"); o_T = sem("o_T"); o_hi = sem("o_hi"); o_lo = sem("o_lo"); o_y = sem("o_y"); o_x = sem("o_x")
        PAIRS = HEADS // 2
        NQ = NT * PAIRS
        q_row = xn32[:, 0:D]
        q_f = xn32[:, D:2 * D]
        q_t = xn32[:, 2 * D:3 * D]
        o_n = xn32[:, 3 * D:4 * D]
        q_hl = xn32[:, 4 * D:5 * D].bitcast(F16).rearrange("p (h n) -> p h n", h=2)
        o_hl = xn32[:, 5 * D:6 * D].bitcast(F16).rearrange("p (h n) -> p h n", h=2)
        q_i = xn32[:, 6 * D:7 * D].bitcast(F16)
        q_iT = [xn32[:, (7 + u) * D:(8 + u) * D].bitcast(F16).rearrange("p (g n) -> p g n", g=4) for u in range(2)]
        small = xn32[:, 9 * D:10 * D].rearrange("p (a h) -> p a h", h=HEADS)
        q_s = [small[:, 2 + u] for u in range(2)]
        q_ns = [small[:, 4 + u] for u in range(2)]
        o_sum = [small[:, 6 + u] for u in range(2)]
        h_mx = [small[:, 8 + u, 0:2] for u in range(2)]
        h_nb = [small[:, 10 + u, 0:2] for u in range(2)]
        h_e = [wk1[:, 2 * u:2 * u + 2] for u in range(2)]
        h_p = [wkh[:, 2 * u:2 * u + 2] for u in range(2)]
        h_T = [wkh[:, 4 + 2 * u:6 + 2 * u] for u in range(2)]

        def attn1_keys_pe(pe):
            for m in range(C):
                last = mm3(PS[:, 6 + m, :], lambda i, c: wa1[:, i, c, 2 * D + m * P:2 * D + (m + 1) * P],
                           lambda j, c: ctxT[:, j, c, :])
            last.then_inc(p_v, 1)
            for t in range(KT):
                mm3(PS[:, t, 0:D], lambda i, c: ctxT[:, i, c, t * P:(t + 1) * P],
                    lambda j, c: wa1[:, j, c, D:2 * D]).then_inc(p_k, 1)
            pe.wait_ge(p_vq, 1)
            for m in range(C):
                for t in range(KT):
                    last = nc.tensor.transpose(PS[:, 6 + m, :].bitcast(F16)[:, t * P:(t + 1) * P],
                                               wkh[:, m, t * P:(t + 1) * P], idh[:, :])
            last.then_inc(p_vT, 1)
            for t in range(KT):
                pe.wait_ge(p_kq, t + 1)
                if t >= 2:
                    pe.wait_ge(p_kd, t - 1)
                for g in range(4):
                    last = nc.tensor.transpose(PS[:, 4 + t % 2, :].bitcast(F16)[:, g * P:(g + 1) * P],
                                               wkh[:, 4 + t, g * P:(g + 1) * P], idh[:, :])
                last.then_inc(p_kT, 1)

        def attn1_keys_act(act):
            act.wait_ge(p_vT, 1)
            for m in range(C):
                last = nc.scalar.activation(Vi[:, :, m * P:(m + 1) * P],
                                            PS[:, 6 + m, :].bitcast(F16)[:, 0:CTX].rearrange("p (t n) -> p t n", n=P),
                                            ACT.Copy)
            last.then_inc(p_vd, 1)
            act.wait_ge(p_zero, 1)
            for t in range(KT):
                act.wait_ge(p_kT, t + 1)
                for f in range(4):
                    r = slice(32 * f, 32 * (f + 1))
                    last = nc.scalar.activation(Kg[r, :, f, t * P:(t + 1) * P],
                                                PS[r, 4 + t % 2, :].bitcast(F16)[:, 0:4 * P].rearrange("p (g n) -> p g n", n=P),
                                                ACT.Copy)
                last.then_inc(p_kd, 1)

        def quantise(dve, x_, y_, s_, r_, n, scale=1.0):
            xg_ = x_.rearrange("p (h d) -> p h d", d=HD)
            nc.vector.tensor_reduce(s_, xg_, AX, ALU.max, apply_absolute_value=True)
            dve.drain()
            nc.vector.tensor_scalar(s_, s_, scale / 127.0, 1e-8, ALU.mult, ALU.max)
            dve.drain()
            nc.vector.reciprocal(r_, s_)
            dve.drain()
            if scale != 1.0:
                nc.vector.tensor_scalar(r_, r_, scale, None, ALU.mult)
                dve.drain()
            nc.vector.tensor_tensor(y_.rearrange("p (h d) -> p h d", d=HD), xg_, bc(r_, HD), ALU.mult)
            dve.drain()

        def attn1_keys_dve(dve):
            nc.vector.memset(Kpad.bitcast(U32), 0).then_inc(p_zero, 1)
            dve.wait_ge(p_v, 1)
            for m in range(C):
                nc.vector.tensor_scalar(wk1[:, m, :], PS[:, 6 + m, :], 1 / SW, bv[:, m:m + 1], ALU.mult, ALU.add)
                dve.drain()
                nc.vector.tensor_reduce(sv[:, m:m + 1], wk1[:, m, :], AX, ALU.max, apply_absolute_value=True)
            dve.drain()
            nc.vector.tensor_scalar(sv[:, :], sv[:, :], 1 / 127.0, 1e-8, ALU.mult, ALU.max)
            dve.drain()
            nc.vector.reciprocal(sm[:, 7, 0:C], sv[:, :])
            dve.drain()
            for m in range(C):
                nc.vector.tensor_scalar(wk1[:, m, :], wk1[:, m, :], sm[:, 7, m:m + 1], MAGIC, ALU.mult, ALU.add)
                dve.drain()
                last = nc.vector.tensor_scalar(wkh[:, m, :], wk1[:, m, :], -MAGIC, None, ALU.add)
            last.then_inc(p_vq, 1)
            for t in range(KT):
                dve.wait_ge(p_k, t + 1)
                kf, ki = wk1[:, 2 + t % 2, 0:D], wk1[:, 2 + t % 2, D:2 * D]
                dve.drain()
                nc.vector.scalar_tensor_tensor(kf, PS[:, t, 0:D], 1 / SW, bk[:, :], ALU.mult, ALU.add)
                dve.drain()
                quantise(dve, kf, ki, sm[:, 8, :], sm[:, 9, :], HEADS)
                nc.vector.tensor_scalar(ki, ki, MAGIC, -MAGIC, ALU.add, ALU.add)
                dve.drain()
                k3 = ki.rearrange("p (h d) -> p h d", d=HD)
                nc.vector.tensor_tensor(k3, k3, bc(sm[:, 8, :], HD), ALU.mult)
                dve.drain()
                kk = wkh[:, 4 + t, :].rearrange("p (h i d) -> p h i d", i=2, d=HD)
                nc.vector.tensor_copy(kk[:, :, 0, :], k3)
                dve.drain()
                nc.vector.tensor_tensor(kk[:, :, 1, :], k3, kk[:, :, 0, :], ALU.subtract).then_inc(p_kq, 1)

        def row_of(base, s, ap):
            if isinstance(base, int):
                return ap[:, base + s]
            v = ap[:, bass.ds(base + s, 1)]
            return v if len(ap.shape) == 2 else v.rearrange("p o d -> p (o d)")

        def attn1_pe(pe):
            attn1_keys_pe(pe)
            meet(pe, 6)

            def queries(tb, ts):
                at_least(pe, q_xn, tb, ts + 1)
                at_least(pe, q_xl, tb, ts)
                for c in range(C):
                    last = nc.tensor.transpose(PS[:, 6, c * P:(c + 1) * P], q_row[:, c * P:(c + 1) * P], idf[:, :])
                last.then_inc(q_xT, 1)
                at_least(pe, q_xl, tb, ts + 1)
                at_least(pe, q_xh, tb, ts + 1)
                mm3(PS[:, 7, 0:D], lambda i, c: q_hl[:, i, c * P:(c + 1) * P],
                    lambda j, c: wa1[:, j, c, 0:D]).then_inc(q_ps, 1)

            def query_transposes(tb, ts):
                at_least(pe, q_int, tb, ts + 1)
                for g in range(4):
                    last = nc.tensor.transpose(PS[:, 7, :].bitcast(F16)[:, g * P:(g + 1) * P],
                                               q_i[:, g * P:(g + 1) * P], idh[:, :])
                last.then_inc(q_T, 1)

            def logits(base, s):
                tb, ts, pair, u = base, s // PAIRS, s % PAIRS, s % 2
                b8 = base * PAIRS
                if pair == 0:
                    at_least(pe, q_ready, tb, ts + 1)
                at_least(pe, h_exp, b8, s - 1)
                at_least(pe, h_max, b8, s - 1)
                for h in range(2):
                    head = 2 * pair + h
                    last = nc.tensor.matmul(PS[:, 2 * u + h, :], q_iT[ts % 2][:, head // 4, :], Kpad[:, head, :],
                                            start=True, stop=True)
                last.then_inc(h_qk, 1)

            def values(base, s):
                b8, u = base * PAIRS, s % 2
                at_least(pe, h_int, b8, s + 1)
                at_least(pe, h_pc, b8, s - 1)
                bank = PS[:, 4 + u, :].bitcast(F16)
                for h in range(2):
                    for k in range(KT):
                        last = nc.tensor.transpose(bank[:, (h * KT + k) * P:(h * KT + k + 1) * P],
                                                   h_p[u][:, h, k * P:(k + 1) * P], idh[:, :])
                last.then_inc(h_pT, 1)

            def weighted(base, s):
                b8, u, pair = base * PAIRS, s % 2, s % PAIRS
                at_least(pe, h_pc, b8, s + 1)
                if pair == 0:
                    at_least(pe, o_norm, base, s // PAIRS)
                pt = h_T[u].rearrange("p a b -> p (a b)")
                for h in range(2):
                    head = 2 * pair + h
                    for k in range(KT):
                        last = nc.tensor.matmul(PS[:, 6, D + head * HD:D + (head + 1) * HD],
                                                pt[:, (h * KT + k) * P:(h * KT + k + 1) * P],
                                                Vi[:, k, head * HD:(head + 1) * HD], start=(k == 0), stop=(k == KT - 1))
                last.then_inc(h_pv, 1)

            def output_transposes(tb, ts):
                at_least(pe, o_norm, tb, ts + 1)
                for c in range(C):
                    last = nc.tensor.transpose(PS[:, 7, c * P:(c + 1) * P], o_n[:, c * P:(c + 1) * P], idf[:, :])
                last.then_inc(o_T, 1)

            def project(tb, ts):
                at_least(pe, o_hi, tb, ts + 1)
                at_least(pe, o_lo, tb, ts + 1)
                at_least(pe, o_x, tb, ts)
                mm3(PS[:, 7, D:2 * D], lambda i, c: o_hl[:, i, c * P:(c + 1) * P],
                    lambda j, c: wa1[:, j, c, 3 * D:4 * D]).then_inc(o_y, 1)

            def step(base, s):
                ts, pair = s // PAIRS, s % PAIRS
                if inside(base * PAIRS, s, 0, NQ):
                    logits(base, s)
                if inside(base * PAIRS, s, 1, NQ + 1):
                    values(base, s - 1)
                if inside(base * PAIRS, s, 2, NQ + 2):
                    weighted(base, s - 2)
                if inside(base, ts, 1, NT + 1):
                    if pair == 2:
                        output_transposes(base, ts - 1)
                    if pair == 3:
                        project(base, ts - 1)
                if inside(base, ts, 0, NT - 1):
                    if pair == 4:
                        queries(base, ts + 1)
                    if pair == 6:
                        query_transposes(base, ts + 1)
            queries(0, 0)
            query_transposes(0, 0)
            tiles(pe, step)
            meet(pe, 7)

        def tiles(eng, step):
            for s in range(2 * PAIRS):
                step(0, s)
            n = (NT - 3) // 2
            with eng.Fori(0, n) as i:
                for s in range(2 * PAIRS, 4 * PAIRS):
                    step(i * 2, s)
            for s in range(2 * PAIRS, (NT - 2 * n) * PAIRS + 4):
                step(2 * n, s)

        def attn1_act(act):
            attn1_keys_act(act)
            meet(act, 6)

            def queries(tb, ts):
                at_least(act, q_xT, tb, ts + 1)
                at_least(act, q_ps, tb, ts)
                nc.scalar.activation(q_hl[:, 0, :], PS[:, 6, 0:D], ACT.Copy).then_inc(q_xh, 1)

            def query_copies(tb, ts):
                at_least(act, q_T, tb, ts + 1)
                nc.scalar.activation(q_iT[ts % 2].rearrange("p g n -> p (g n)"), PS[:, 7, :].bitcast(F16)[:, 0:2 * D],
                                     ACT.Copy).then_inc(q_ready, 1)

            def exponentials(base, s):
                b8, u, pair = base * PAIRS, s % 2, s % PAIRS
                v = (s // PAIRS) % 2
                at_least(act, h_max, b8, s + 1)
                at_least(act, h_int, b8, s - 1)
                for h in range(2):
                    head = 2 * pair + h
                    last = nc.scalar.activation(h_e[u][:, h, :], PS[:, 2 * u + h, :], ACT.Exp, bias=h_nb[u][:, h:h + 1],
                                                scale=q_s[v][:, head:head + 1], accum_out=o_sum[v][:, head:head + 1])
                last.then_inc(h_exp, 1)

            def copies(base, s):
                b8, u = base * PAIRS, s % 2
                at_least(act, h_pT, b8, s + 1)
                at_least(act, h_pv, b8, s - 1)
                nc.scalar.activation(h_T[u].rearrange("p a b -> p (a b)"), PS[:, 4 + u, :].bitcast(F16),
                                     ACT.Copy).then_inc(h_pc, 1)

            def output_high(tb, ts):
                at_least(act, o_T, tb, ts + 1)
                at_least(act, o_y, tb, ts)
                for c in range(C):
                    last = nc.scalar.activation(o_hl[:, 0, c * P:(c + 1) * P], PS[:, 7, c * P:(c + 1) * P], ACT.Copy,
                                                scale=sv[:, c:c + 1])
                last.then_inc(o_hi, 1)

            def step(base, s):
                ts, pair = s // PAIRS, s % PAIRS
                if inside(base * PAIRS, s, 0, NQ):
                    exponentials(base, s)
                if inside(base * PAIRS, s, 1, NQ + 1):
                    copies(base, s - 1)
                if inside(base, ts, 1, NT + 1) and pair == 2:
                    output_high(base, ts - 1)
                if inside(base, ts, 0, NT - 1):
                    if pair == 4:
                        queries(base, ts + 1)
                    if pair == 6:
                        query_copies(base, ts + 1)
            queries(0, 0)
            query_copies(0, 0)
            tiles(act, step)
            meet(act, 7)

        def attn1_dve(dve):
            attn1_keys_dve(dve)
            meet(dve, 6)
            dve.wait_ge(rstd_ready, 3)

            def queries(tb, ts):
                at_least(dve, q_xT, tb, ts)
                nc.vector.tensor_scalar(q_row, row_of(tb, ts, x_sb), row_of(tb, ts, mv)[:, 0:1],
                                        row_of(tb, ts, rstd)[:, 0:1] if not isinstance(tb, int) else rstd[:, tb + ts:tb + ts + 1],
                                        ALU.subtract, ALU.mult).then_inc(q_xn, 1)

            def queries_low(tb, ts):
                at_least(dve, q_xh, tb, ts + 1)
                at_least(dve, q_ps, tb, ts)
                nc.vector.tensor_tensor(q_hl[:, 1, :], PS[:, 6, 0:D], q_hl[:, 0, :], ALU.subtract).then_inc(q_xl, 1)

            def query_integers(tb, ts):
                v = ts % 2
                at_least(dve, q_ps, tb, ts + 1)
                nc.vector.scalar_tensor_tensor(q_f, PS[:, 7, 0:D], 1 / SW, bq[:, :], ALU.mult, ALU.add)
                dve.drain()
                at_least(dve, h_exp, tb * PAIRS, (ts - 1) * PAIRS)
                quantise(dve, q_f, q_t, q_s[v], small[:, 0], HEADS, 0.25)
                nc.vector.tensor_scalar(q_ns[v], q_s[v], -1.0, None, ALU.mult)
                at_least(dve, q_T, tb, ts)
                nc.vector.tensor_scalar(q_i.rearrange("p (h i d) -> p h i d", i=2, d=HD),
                                        q_t.rearrange("p (h d) -> p h d", d=HD).unsqueeze(2).broadcast_to([P, HEADS, 2, HD]),
                                        MAGIC, -MAGIC, ALU.add, ALU.add).then_inc(q_int, 1)

            def maxima(base, s):
                b8, u, pair = base * PAIRS, s % 2, s % PAIRS
                v = (s // PAIRS) % 2
                at_least(dve, h_qk, b8, s + 1)
                at_least(dve, h_exp, b8, s - 1)
                nc.vector.tensor_reduce(h_mx[u], PS[:, 2 * u:2 * u + 2, :], AX, ALU.max)
                dve.drain()
                nc.vector.tensor_tensor(h_nb[u], h_mx[u], q_ns[v][:, 2 * pair:2 * pair + 2], ALU.mult)
                dve.drain()
                nc.vector.tensor_scalar(h_nb[u], h_nb[u], LN255, None, ALU.add).then_inc(h_max, 1)

            def integers(base, s):
                b8, u = base * PAIRS, s % 2
                at_least(dve, h_exp, b8, s + 1)
                at_least(dve, h_pT, b8, s - 1)
                nc.vector.tensor_scalar(h_p[u], h_e[u], MAGIC, -MAGIC, ALU.add, ALU.add).then_inc(h_int, 1)

            def normalised(tb, ts):
                v = ts % 2
                at_least(dve, h_pv, tb * PAIRS, (ts + 1) * PAIRS)
                at_least(dve, o_T, tb, ts)
                nc.vector.reciprocal(small[:, 1], o_sum[v])
                dve.drain()
                nc.vector.tensor_tensor(o_n.rearrange("p (h d) -> p h d", d=HD),
                                        PS[:, 6, D:2 * D].rearrange("p (h d) -> p h d", d=HD), bc(small[:, 1], HD),
                                        ALU.mult).then_inc(o_norm, 1)

            def output_low(tb, ts):
                at_least(dve, o_hi, tb, ts + 1)
                at_least(dve, o_y, tb, ts)
                for c in range(C):
                    last = nc.vector.scalar_tensor_tensor(o_hl[:, 1, c * P:(c + 1) * P], PS[:, 7, c * P:(c + 1) * P],
                                                          sv[:, c:c + 1], o_hl[:, 0, c * P:(c + 1) * P],
                                                          ALU.mult, ALU.subtract)
                last.then_inc(o_lo, 1)

            def update(tb, ts):
                at_least(dve, o_y, tb, ts + 1)
                xt = row_of(tb, ts, x_sb)
                nc.vector.scalar_tensor_tensor(xt, PS[:, 7, D:2 * D], tgw[:, 1:2], xt, ALU.mult, ALU.add)
                dve.drain()
                nc.vector.tensor_tensor(xt, xt, bp[:, :], ALU.add).then_inc(o_x, 1)
                dve.drain()
                nc.vector.bn_stats(bst[:, :], xt)
                dve.drain()
                nc.vector.bn_aggr(mv1[:, :], bst[:, :])
                dve.drain()
                nc.vector.tensor_copy(row_of(tb, ts, mv), mv1[:, :])

            def step(base, s):
                ts, pair = s // PAIRS, s % PAIRS
                if inside(base * PAIRS, s, 0, NQ):
                    maxima(base, s)
                if inside(base * PAIRS, s, 1, NQ + 1):
                    integers(base, s - 1)
                if inside(base, ts, 1, NT + 1):
                    if pair == 2:
                        normalised(base, ts - 1)
                    if pair == 3:
                        output_low(base, ts - 1)
                        update(base, ts - 1)
                if inside(base, ts, 0, NT - 1):
                    if pair == 3:
                        queries(base, ts + 1)
                    if pair == 4:
                        queries_low(base, ts + 1)
                    if pair == 5:
                        query_integers(base, ts + 1)
            queries(0, 0)
            queries_low(0, 0)
            query_integers(0, 0)
            tiles(dve, step)
            stats_end(3)
            meet(dve, 7)

        @block.sync
        def _(sp):
            sp.dma_start(ctxf.rearrange("p (c n) -> p c n", c=C),
                         a["ctxT"].rearrange("(c p) n -> p c n", c=C)).then_inc(ld_ctx, 16)
            sp.dma_start(w0f.rearrange("p (c n) -> p c n", c=C),
                         a["wa0"].rearrange("(c p) n -> p c n", c=C)).then_inc(ld_w0, 16)
            sp.dma_start(x_sb[:, :, :], a["x"].rearrange("(t p) d -> p t d", p=P)).then_inc(ld_x, 16)
            sp.dma_start(g4[:, 0:2], a["g_xattn"].rearrange("(o n) -> o n", o=1).broadcast_to([P, 2])).then_inc(ld_small, 16)
            sp.dma_start(g4[:, 2:4], a["g_ffn"].rearrange("(o n) -> o n", o=1).broadcast_to([P, 2])).then_inc(ld_small, 16)
            for dst, name in ((bq, "bq"), (bk, "bk"), (bp, "bp")):
                sp.dma_start(dst[:, :], a[name].rearrange("(o n) -> o n", o=1).broadcast_to([P, D])).then_inc(ld_small, 16)
            sp.dma_start(bv[:, :], a["bvT"]).then_inc(ld_small, 16)
            sp.dma_start(bg[:, :], a["bgT"]).then_inc(ld_small, 16)
            sp.dma_start(w1f.rearrange("p (c n) -> p c n", c=C),
                         a["wa1"].rearrange("(c p) n -> p c n", c=C)).then_inc(ld_w1, 16)
            for l in range(2):
                sp.dma_start(rwf[l].rearrange("p (c n) -> p c n", c=C),
                             a[f"rw{l}"].rearrange("(c p) n -> p c n", c=C)).then_inc(ld_rw, 16)
            if stage >= 3:
                sp.wait_ge(const_ready, 1)
                for l in range(2):
                    v = xs[l].rearrange("(p r) d -> p r d", p=P)
                    sp.dma_start(v, zero[:, :].unsqueeze(1).broadcast_to([P, NS[l], D])).then_inc(zeroed[l], 16)

            def load(slot, rounds, src, cols, rows=P):
                at_least(sp, stg_split[slot], *rounds)
                sp.dma_start(stg[0:rows, slot, 0:cols].rearrange("p (c n) -> p c n", n=src.shape[-1]), src)\
                    .then_inc(stg_loaded[slot], 16)

            def load_layer(l, r0):
                g = a[f"sgu{l}"].rearrange("(c p) n -> p c n", c=C)
                for n in range(4):
                    load(n, (r0, 0), g[:, n // 2:n // 2 + 1, (n % 2) * (SG // 2):(n % 2 + 1) * (SG // 2)], SG // 2)
                d = a[f"sdn{l}"][0:SFULL * P, :].rearrange("(c p) n -> p c n", p=P)
                load(0, (r0, 1), d[:, 0:2, :], 2 * D)
                load(1, (r0, 1), d[:, 2:4, :], 2 * D)
                load(2, (r0, 1), d[:, 4:5, :], D)
                load(3, (r0, 1), a[f"sdn{l}"][SFULL * P:, :].unsqueeze(1), D, SREM)

                def two_experts(base, s):
                    for k in range(2):
                        e = base * 2 + 2 * s + k if isinstance(base, int) else bass.ds(base * 2 + (2 * s + k), 1)
                        ge = a[f"gu{l}"][e] if isinstance(base, int) else a[f"gu{l}"][e, :, :].rearrange("o h n -> (o h) n")
                        de = a[f"dn{l}"][e] if isinstance(base, int) else a[f"dn{l}"][e, :, :].rearrange("o h n -> (o h) n")
                        load(2 * k, (base, r0 + 2 + s), ge.rearrange("(c p) n -> p c n", c=C), 2 * EG)
                        load(2 * k + 1, (base, r0 + 2 + s), de.rearrange("(c p) n -> p c n", c=2), 2 * D, EC)
                steps(sp, E[l] // 2, 1, 0, 0, two_experts)

            if stage >= 3:
                load_layer(0, 0)
                ffn_dma(sp, 0)
            if stage >= 6:
                load_layer(1, 2 + E[0] // 2)
                ffn_dma(sp, 1)
                for t in range(NT):
                    at_least(sp, c_used[1], 0, TOPK[1] * (t + 1))
                    sp.dma_start(out.rearrange("(t p) d -> t p d", p=P)[t], x_sb[:, t, :]).then_inc(out_done, 16)
                sp.wait_ge(out_done, 16 * NT)
            else:
                sp.wait_ge(phase, 3 * {0: 1, 1: 2, 2: 3, 3: 5, 4: 7, 5: 8}[stage])
                sp.dma_start(out.rearrange("(t p) d -> p t d", p=P), x_sb[:, :, :]).then_inc(out_done, 16)
                sp.wait_ge(out_done, 16)

        def split_on_pool(pl, slot, seen, cols, hi, lo, rows=P):
            pl.wait_ge(stg_loaded[slot], seen)
            w = stg[0:rows, slot, 0:cols]
            s = swb[0:rows, 0:1].broadcast_to([rows, cols])
            nc.gpsimd.tensor_tensor(hi, w, s, ALU.mult)
            nc.gpsimd.tensor_tensor(w, w, s, ALU.mult)
            pl.drain()
            return nc.gpsimd.tensor_tensor(lo, w, hi, ALU.subtract).then_inc(stg_split[slot], 1)

        def split_layer(pl, l, r0):
            if l == 1:
                pl.wait_ge(shared_used, 1)
            for n in range(4):
                cols = slice((n % 2) * (SG // 2), (n % 2 + 1) * (SG // 2))
                split_on_pool(pl, n, 16 * (r0 + 1), SG // 2, sgu[:, 0, n // 2, cols], sgu[:, 1, n // 2, cols])
            for n in range(2):
                split_on_pool(pl, n, 16 * (r0 + 2), 2 * D, sdn[:, 0, 2 * n:2 * n + 2, :].rearrange("p c n -> p (c n)"),
                              sdn[:, 1, 2 * n:2 * n + 2, :].rearrange("p c n -> p (c n)"))
            split_on_pool(pl, 2, 16 * (r0 + 2), D, sdn[:, 0, 4, :], sdn[:, 1, 4, :])
            split_on_pool(pl, 3, 16 * (r0 + 2), D, sdn[0:SREM, 0, 5, :], sdn[0:SREM, 1, 5, :], SREM)
            pl.drain().then_inc(shared_ready[l], 1)

            if l == 1:
                pl.wait_ge(experts_used, 1)
            for e in range(E[l]):
                k, seen = e % 2, 16 * (r0 + 3 + e // 2)
                split_on_pool(pl, 2 * k, seen, 2 * EG, GU[l][:, e, 0].rearrange("p c n -> p (c n)"),
                              GU[l][:, e, 1].rearrange("p c n -> p (c n)"))
                split_on_pool(pl, 2 * k + 1, seen, 2 * D, DN[l][:, e, 0].rearrange("p c n -> p (c n)"),
                              DN[l][:, e, 1].rearrange("p c n -> p (c n)"), EC)
            pl.drain().then_inc(experts_ready[l], 1)

        @block.gpsimd
        def _(pl):
            nc.gpsimd.memset(zero[:, :], 0.0).then_inc(const_ready, 1)
            nc.gpsimd.memset(swb[:, :], SW)
            nc.gpsimd.memset(mhalf[:, :], -0.5)
            nc.gpsimd.memset(idf[:, :], 0.0)
            nc.gpsimd.memset(ones_h[:, :], 1.0)
            nc.gpsimd.memset(headmask[:, :], 1.0)
            nc.gpsimd.memset(lower[:, :, :], 1.0)
            nc.gpsimd.memset(selm[:, :, :], 0.0)
            nc.gpsimd.iota(texp[:, :], pattern=[[1, max(NS)]], base=0, channel_multiplier=0)
            pl.drain()
            nc.gpsimd.affine_select(out=idf[:, :], in_=idf[:, :], compare_op=ALU.not_equal, fill=1.0, base=0,
                                    pattern=[[-1, P]], channel_multiplier=1)
            nc.gpsimd.affine_select(out=tri[:, :], in_=ones_h[:, :], compare_op=ALU.is_gt, fill=0.0, base=0,
                                    pattern=[[1, P]], channel_multiplier=-1)
            hm = headmask[:, :].rearrange("p (b d) -> p b d", d=HD)
            nc.gpsimd.affine_select(out=hm, in_=hm, compare_op=ALU.is_ge, fill=0.0, base=0,
                                    pattern=[[-HD, P // HD], [0, HD]], channel_multiplier=1)
            nc.gpsimd.affine_select(out=lower[:, :, :], in_=lower[:, :, :], compare_op=ALU.is_gt, fill=0.0, base=0,
                                    pattern=[[1, 16], [-1, 16]], channel_multiplier=0)
            nc.gpsimd.tensor_copy(tileno[:, :], texp[:, :])
            pl.drain()
            nc.gpsimd.affine_select(out=hm, in_=hm, compare_op=ALU.is_ge, fill=0.0, base=HD - 1,
                                    pattern=[[HD, P // HD], [0, HD]], channel_multiplier=-1)
            nc.gpsimd.tensor_copy(idh[:, :], idf[:, :])
            pl.drain().then_inc(const_ready, 1)
            for n in range(1 if stage < 2 else 2 if stage < 4 else 3 if stage < 5 else 4):
                if n == 1 and stage >= 3:
                    split_layer(pl, 0, 0)
                if n == 2:
                    ffn_pool(pl, 0)
                if n == 3 and stage >= 6:
                    split_layer(pl, 1, 2 + E[0] // 2)
                pl.wait_ge(stats_ready, n + 1)
                nc.gpsimd.tensor_tensor(rstd[:, :], ve[:, :], mhalf[:, :], ALU.pow).then_inc(rstd_ready, 1)
            if stage == 3:
                ffn_pool(pl, 0)
            if stage >= 6:
                ffn_pool(pl, 1)

        @block.scalar
        def _(act):
            act.wait_ge(ld_ctx, 16)
            nc.scalar.activation(ctxT[:, 0].rearrange("p c n -> p (c n)"), ctxf, ACT.Copy).then_inc(hi_done, 1)
            act.wait_ge(ld_w0, 16)
            nc.scalar.activation(wa0[:, 0].rearrange("p c n -> p (c n)"), w0f, ACT.Copy, scale=SW).then_inc(hi_done, 1)
            act.wait_ge(ld_w1, 16)
            nc.scalar.activation(wa1[:, 0].rearrange("p c n -> p (c n)"), w1f, ACT.Copy, scale=SW).then_inc(hi_done, 1)
            act.wait_ge(ld_rw, 32)
            for l in range(2):
                nc.scalar.activation(rw[l][:, 0].rearrange("p c n -> p (c n)"), rwf[l], ACT.Copy, scale=SW).then_inc(hi_done, 1)
            act.wait_ge(ld_small, 112)
            nc.scalar.activation(tg[:, :], g4[:, :], ACT.Tanh).then_inc(tg_ready, 1)
            for t in range(KT):
                u = t % 2
                act.wait_ge(kv_ps, t + 1)
                if t >= 2:
                    act.wait_ge(sum_ps, t - 1)
                nc.scalar.activation(wk1[:, 2 * u, 0:D], PS[:, u, 0:D], ACT.Exp, scale=1 / SW)
                nc.scalar.activation(wk1[:, 2 * u, D:2 * D], PS[:, u, 0:D], ACT.Relu, scale=1 / SW)
                nc.scalar.activation(wkh[:, 2 * u, 0:D], PS[:, u, D:2 * D], ACT.Copy, scale=1 / SW).then_inc(kv_parts, 1)
                act.wait_ge(kv_k, t + 1)
                nc.scalar.activation(wkh[:, 2 * u + 1, 0:D], wk1[:, 2 * u + 1, 0:D], ACT.Copy).then_inc(kv_kh, 1)
                for b in (2 * t, 2 * t + 1):
                    act.wait_ge(sum_f, b + 1)
                    nc.scalar.activation(KV[:, 0, b].rearrange("p m k e -> p (m k e)"), la_t[b % 2],
                                         ACT.Copy).then_inc(sum_hi, 1)
            meet(act, 1)
            if stage >= 1:
                def batch(base, s):
                    u = s % 2
                    if inside(base, s, 0, NB):
                        at_least(act, a_xT, base, s + 1)
                        nc.scalar.activation(la_xh, PS[:, 0, :], ACT.Copy).then_inc(a_xh, 1)
                        at_least(act, a_qg, base, s + 1)
                        at_least(act, a_phi, base, s)
                        nc.scalar.activation(la_e, PS[:, 1, :], ACT.Exp, scale=1 / SW)
                        nc.scalar.activation(la_r, PS[:, 1, :], ACT.Relu, scale=1 / SW)
                        at_least(act, a_og, base, s - 1)
                        for m in range(C):
                            last = nc.scalar.activation(la_t[u][:, m * TB:(m + 1) * TB], PS[:, 2, m * TB:(m + 1) * TB],
                                                        ACT.Tanh, bias=bg[:, m:m + 1], scale=0.5 / SW)
                        last.then_inc(a_act, 1)
                        at_least(act, a_phi, base, s + 1)
                        at_least(act, a_nd, base, s)
                        nc.scalar.activation(la_ph, la_phi, ACT.Copy).then_inc(a_phih, 1)
                    if inside(base, s, 1, NB + 1):
                        at_least(act, a_nd, base, s)
                        at_least(act, a_og, base, s - 1)
                        nc.scalar.activation(la_den, PS[:, 4, :], ACT.Identity, bias=z_eps[:, 0:1]).then_inc(a_den, 1)
                        at_least(act, a_og, base, s)
                        at_least(act, a_out, base, s - 1)
                        nc.scalar.activation(la_oh, la_og, ACT.Copy).then_inc(a_ogh, 1)
                steps(act, NB + 1, 2, 2, 1, batch)
                meet(act, 2)
            if stage >= 2:
                route_act(act, 0)
            if stage >= 3:
                ffn_act(act, 0)
            if stage >= 4:
                attn1_act(act)
            if stage >= 5:
                route_act(act, 1)
            if stage >= 6:
                ffn_act(act, 1)

        @block.vector
        def _(dve):
            nc.vector.memset(z_eps[:, :], Z_EPS)
            dve.wait_ge(hi_done, 1)
            nc.vector.tensor_tensor(ctxT[:, 1].rearrange("p c n -> p (c n)"), ctxf,
                                    ctxT[:, 0].rearrange("p c n -> p (c n)"), ALU.subtract).then_inc(lo_done, 1)
            for n, (w, f) in enumerate(((wa0, w0f), (wa1, w1f), (rw[0], rwf[0]), (rw[1], rwf[1]))):
                dve.wait_ge(hi_done, n + 2)
                nc.vector.scalar_tensor_tensor(w[:, 1].rearrange("p c n -> p (c n)"), f, SW,
                                               w[:, 0].rearrange("p c n -> p (c n)"), ALU.mult, ALU.subtract)\
                    .then_inc(lo_done, 1)
            dve.wait_ge(tg_ready, 1)
            nc.vector.tensor_scalar(tgw[:, :], tg[:, :], 1 / SW, None, ALU.mult)
            nc.vector.tensor_scalar(bg[:, :], bg[:, :], 0.5, None, ALU.mult)
            nc.vector.tensor_scalar(bp[:, :], bp[:, :], tg[:, 1:2], None, ALU.mult)
            dve.drain()
            nc.vector.tensor_scalar(tg[:, 0:1], tgw[:, 0:1], 0.5, None, ALU.mult).then_inc(tgw_ready, 1)
            dve.wait_ge(const_ready, 2)
            for t in range(KT):
                u = t % 2
                dve.wait_ge(kv_parts, t + 1)
                nc.vector.scalar_tensor_tensor(wk1[:, 2 * u + 1, 0:D], wk1[:, 2 * u, 0:D], 1.0, wk1[:, 2 * u, D:2 * D],
                                               ALU.min, ALU.add).then_inc(kv_k, 1)
                nc.vector.scalar_tensor_tensor(wkh[:, 2 * u, D:2 * D], PS[:, u, D:2 * D], 1 / SW, wkh[:, 2 * u, 0:D],
                                               ALU.mult, ALU.subtract)
                dve.wait_ge(kv_kh, t + 1)
                nc.vector.tensor_tensor(wkh[:, 2 * u + 1, D:2 * D], wk1[:, 2 * u + 1, 0:D], wkh[:, 2 * u + 1, 0:D],
                                        ALU.subtract).then_inc(kv_kl, 1)
                dve.wait_ge(sum_ps, t + 1)
                for b in (2 * t, 2 * t + 1):
                    f = la_t[b % 2].rearrange("p (k e) -> p k e", e=P)
                    nc.vector.tensor_tensor(f, PS[:, 2 + 2 * u + b % 2, :].rearrange("p (k e) -> p k e", e=P),
                                            headmask[:, :].unsqueeze(1).broadcast_to([P, 4, P]), ALU.mult).then_inc(sum_f, 1)
                    dve.wait_ge(sum_hi, b + 1)
                    nc.vector.tensor_tensor(KV[:, 1, b].rearrange("p m k e -> p (m k e)"), la_t[b % 2],
                                            KV[:, 0, b].rearrange("p m k e -> p (m k e)"), ALU.subtract)
            dve.wait_ge(ld_x, 16)
            for t in range(NT):
                dve.drain()
                stats(t)
            stats_end(0)
            meet(dve, 1)
            if stage >= 1:
                dve.wait_ge(rstd_ready, 1)

                def normalise(base, s):
                    at_least(dve, a_xT, base, s - 1)
                    for i in range(2):
                        row = 2 * (s % 2) + i
                        if isinstance(base, int):
                            t = 2 * (base + s) + i
                            xt, m, r = x_sb[:, t, :], mv[:, t, 0:1], rstd[:, t:t + 1]
                        else:
                            t = bass.ds(base * 2 + (2 * s + i), 1)
                            xt, m, r = x_sb[:, t, :].rearrange("p o d -> p (o d)"), mv[:, t, 0], rstd[:, t]
                        last = nc.vector.tensor_scalar(xnf[:, row, :], xt, m, r, ALU.subtract, ALU.mult)
                    last.then_inc(a_xn, 1)

                def batch(base, s):
                    if inside(base, s, 0, NB):
                        at_least(dve, a_xh, base, s + 1)
                        at_least(dve, a_qg, base, s)
                        nc.vector.tensor_tensor(la_xl, PS[:, 0, :], la_xh, ALU.subtract).then_inc(a_xl, 1)
                        if inside(base, s, 0, NB - 1):
                            normalise(base, s + 1)
                        at_least(dve, a_act, base, s + 1)
                        at_least(dve, a_phih, base, s)
                        nc.vector.scalar_tensor_tensor(la_phi, la_e, 1.0, la_r, ALU.min, ALU.add).then_inc(a_phi, 1)
                        at_least(dve, a_phih, base, s + 1)
                        at_least(dve, a_nd, base, s)
                        nc.vector.tensor_tensor(la_pl, la_phi, la_ph, ALU.subtract).then_inc(a_phil, 1)
                    if inside(base, s, 1, NB + 1):
                        at_least(dve, a_den, base, s)
                        nc.vector.reciprocal(la_den, la_den)
                        dve.drain()
                        nc.vector.tensor_tensor(la_den, PS[:, 3, :], la_den, ALU.mult)
                        dve.drain()
                        at_least(dve, a_ogh, base, s - 1)
                        nc.vector.scalar_tensor_tensor(la_og, la_t[(s - 1) % 2], 1.0, la_den, ALU.add, ALU.mult)\
                            .then_inc(a_og, 1)
                        at_least(dve, a_ogh, base, s)
                        at_least(dve, a_out, base, s - 1)
                        nc.vector.tensor_tensor(la_ol, la_og, la_oh, ALU.subtract).then_inc(a_ogl, 1)
                        at_least(dve, a_out, base, s)
                        b = base + (s - 1) if isinstance(base, int) else None
                        for i in range(2):
                            t = 2 * b + i if b is not None else bass.ds(base * 2 + (2 * (s - 1) + i), 1)
                            xt = x_sb[:, t, :] if b is not None else x_sb[:, t, :].rearrange("p o d -> p (o d)")
                            last = nc.vector.scalar_tensor_tensor(xt, PS[:, 5, i * D:(i + 1) * D], tg[:, 0:1], xt,
                                                                  ALU.mult, ALU.add)
                            if i == 1:
                                last.then_inc(a_x, 1)
                        dve.drain()
                        for i in range(2):
                            t = 2 * b + i if b is not None else bass.ds(base * 2 + (2 * (s - 1) + i), 1)
                            stats(t)
                            dve.drain()
                normalise(0, 0)
                steps(dve, NB + 1, 2, 2, 2, batch)
                stats_end(1)
                meet(dve, 2)
            if stage >= 2:
                route_dve(dve, 0)
            if stage >= 3:
                ffn_dve(dve, 0)
            if stage >= 4:
                attn1_dve(dve)
            if stage >= 5:
                route_dve(dve, 1)
            if stage >= 6:
                ffn_dve(dve, 1)

        @block.tensor
        def _(pe):
            pe.wait_ge(lo_done, 2)
            pe.wait_ge(const_ready, 2)

            def keys_values(t):
                last = mm3(PS[:, t % 2, :], lambda i, c: ctxT[:, i, c, t * P:(t + 1) * P],
                           lambda j, c: wa0[:, j, c, 2 * D:4 * D])
                last.then_inc(kv_ps, 1)
            keys_values(0)
            for t in range(KT):
                u = t % 2
                if t + 1 < KT:
                    if t >= 1:
                        pe.wait_ge(kv_kl, t)
                    keys_values(t + 1)
                pe.wait_ge(kv_kl, t + 1)
                if t >= 2:
                    pe.wait_ge(sum_f, 2 * (t - 1))
                for b in (2 * t, 2 * t + 1):
                    r = slice(SB_ * (b % 2), SB_ * (b % 2 + 1))
                    for m in range(C):
                        km = [wkh[r, 2 * u + 1, i * D + m * P:i * D + (m + 1) * P] for i in range(2)]
                        vm = [wkh[r, 2 * u, i * D + m * P:i * D + (m + 1) * P] for i in range(2)]
                        bank = PS[:, 2 + 2 * u + b % 2, m * 2 * P:(m + 1) * 2 * P]
                        for n, (i, j) in enumerate(HL):
                            nc.tensor.matmul(bank[:, 0:P], km[i], vm[j], start=(n == 0), stop=(n == 2))
                        for i in range(2):
                            last = nc.tensor.matmul(bank[:, P:2 * P], km[i], ones_h[r, :], start=(i == 0), stop=(i == 1))
                last.then_inc(sum_ps, 1)
            meet(pe, 1)
            if stage >= 1:
                def batch(base, s):
                    def front_t():
                        at_least(pe, a_xn, base, s + 1)
                        at_least(pe, a_xl, base, s)
                        for i in range(2):
                            for c in range(C):
                                last = nc.tensor.transpose(PS[:, 0, c * TB + i * P:c * TB + (i + 1) * P],
                                                           xnf[:, 2 * (s % 2) + i, c * P:(c + 1) * P], idf[:, :])
                        last.then_inc(a_xT, 1)

                    if inside(base, s, 0, NB):
                        front_t()
                    if inside(base, s, 1, NB + 1):
                        at_least(pe, a_phil, base, s)
                        at_least(pe, a_og, base, s - 1)
                        at_least(pe, a_den, base, s - 1)
                        for k in range(2):
                            for m in range(C):
                                for n, (i, j) in enumerate(HL):
                                    b = base + (s - 1) if isinstance(base, int) else bass.ds(base + (s - 1), 1)
                                    w = KV[:, i, b, m, k, :]
                                    if not isinstance(base, int):
                                        w = w.rearrange("p o e -> p (o e)")
                                    last = nc.tensor.matmul(PS[:, 3 + k, m * TB:(m + 1) * TB], w,
                                                            (la_ph, la_pl)[j][:, m * TB:(m + 1) * TB],
                                                            start=(n == 0), stop=(n == 2))
                        last.then_inc(a_nd, 1)
                    if inside(base, s, 0, NB):
                        at_least(pe, a_xh, base, s + 1)
                        at_least(pe, a_xl, base, s + 1)
                        at_least(pe, a_act, base, s)
                        for k in range(2):
                            for m in range(C):
                                last = mm3(PS[:, 1 + k, m * TB:(m + 1) * TB],
                                           lambda i, c: wa0[:, i, c, k * D + m * P:k * D + (m + 1) * P],
                                           lambda j, c: (la_xh, la_xl)[j][:, c * TB:(c + 1) * TB])
                        last.then_inc(a_qg, 1)
                    if inside(base, s, 1, NB + 1):
                        at_least(pe, a_ogl, base, s)
                        at_least(pe, a_x, base, s - 1)
                        for i in range(2):
                            last = mm3(PS[:, 5, i * D:(i + 1) * D],
                                       lambda h, c: (la_oh, la_ol)[h][:, c * TB + i * P:c * TB + (i + 1) * P],
                                       lambda h, c: wa0[:, h, c, 4 * D:5 * D])
                        last.then_inc(a_out, 1)
                steps(pe, NB + 1, 2, 2, 1, batch)
                meet(pe, 2)
            if stage >= 2:
                route_pe(pe, 0)
            if stage >= 3:
                ffn_pe(pe, 0)
            if stage >= 4:
                attn1_pe(pe)
            if stage >= 5:
                route_pe(pe, 1)
            if stage >= 6:
                ffn_pe(pe, 1)


_INS = ["x", "ctxT", "wa0", "wa1", "rw0", "rw1", "gu0", "gu1", "dn0", "dn1", "sgu0", "sgu1", "sdn0", "sdn1",
        "g_xattn", "g_ffn", "bq", "bk", "bp", "bvT", "bgT"]


def laid_out(inputs):
    import numpy as np
    v = {k: np.asarray(a) for k, a in inputs.items()}
    n = {}
    n["x"] = v["x"].reshape(-1, v["x"].shape[-1])
    n["ctxT"] = v["ctx_2048"].reshape(-1, v["ctx_2048"].shape[-1]).T
    n["wa0"] = np.concatenate([v["L0_xattn_Wq"].T, v["L0_xattn_Wg"].T, v["L0_xattn_Wkv"].T, v["L0_xattn_Wo"].T], 1)
    n["wa1"] = np.concatenate([v["L1_xattn_Wq"], v["L1_xattn_Wkv"], v["L1_xattn_Wp"]], 1)
    n["rw0"] = np.concatenate([v["L0_ffn_router_w"].T, v["L0_ffn_shared_gate_w"][:, None]], 1)
    n["rw1"] = np.concatenate([v["L1_ffn_router_w"].T, v["L1_ffn_se_gate_w"].T], 1)
    n["gu0"] = np.concatenate([v["L0_ffn_w_gate"], v["L0_ffn_w_up"]], 2)
    n["dn0"] = v["L0_ffn_w_down"]
    n["gu1"] = np.concatenate([v["L1_ffn_gate_w"].transpose(0, 2, 1), v["L1_ffn_up_w"].transpose(0, 2, 1)], 2)
    n["dn1"] = v["L1_ffn_down_w"].transpose(0, 2, 1)
    for l, (g, u, d) in enumerate(((v["L0_ffn_sw_gate"], v["L0_ffn_sw_up"], v["L0_ffn_sw_down"]),
                                   (v["L1_ffn_shared_gate_w"].T, v["L1_ffn_shared_up_w"].T, v["L1_ffn_shared_down_w"].T))):
        cuts = range(0, g.shape[1], 128)
        n[f"sgu{l}"] = np.concatenate([w[:, c:c + 128] for c in cuts for w in (g, u)], 1)
        n[f"sdn{l}"] = d
    n["g_xattn"], n["g_ffn"] = v["g_xattn"], v["g_ffn"]
    n["bq"], n["bp"] = v["L1_xattn_bq"], v["L1_xattn_bp"]
    n["bk"], bv = np.split(v["L1_xattn_bkv"], 2)
    n["bvT"] = bv.reshape(2, 128).T
    n["bgT"] = v["L0_xattn_bg"].reshape(2, 128).T
    return {k: np.ascontiguousarray(n[k]) for k in _INS}


def kernel(**inputs):
    import concourse.bacc as _bacc
    from concourse import mybir as _mybir
    from concourse.bass_utils import run_bass_kernel_spmd as _run

    nc = _bacc.Bacc("TRN2", target_bir_lowering=False, num_devices=1)
    arrays = laid_out(inputs)
    aps = {k: nc.dram_tensor(k, v.shape, _mybir.dt.from_np(v.dtype), kind="ExternalInput").ap()
           for k, v in arrays.items()}
    shape = inputs["x"].shape
    out = nc.dram_tensor("out", (shape[0] * shape[1], shape[2]), _mybir.dt.float32, kind="ExternalOutput").ap()
    gated_flamingo(nc, aps, out)
    r = _run(nc, [arrays], core_ids=[0])
    return r.results[0]["out"].reshape(shape)
```

```python
from contextlib import ExitStack

import concourse.bass as bass
from concourse import mybir

F32 = mybir.dt.float32
F16 = mybir.dt.float16
I32 = mybir.dt.int32
U32 = mybir.dt.uint32
ACT = mybir.ActivationFunctionType
ALU = mybir.AluOpType
AX = mybir.AxisListType.X

P = 128
D = 256
C = D // P
HEADS, HD = 16, 16
MAGIC = 1.5 * 2.0 ** 23
SW = 256.0
LN255 = 5.541263545158426
LN_EPS = 1e-5
Z_EPS = 1e-6
HL = ((0, 0), (0, 1), (1, 0))


class Count:

    def __init__(self, sem, start):
        self.sem, self.start = sem, start


def gated_flamingo(nc, a, out, stage=99):
    T = a["x"].shape[0]
    NT = T // P
    CTX = a["ctxT"].shape[1]
    NB = 8
    TB = T // NB
    SB_ = CTX // NB
    KT = CTX // P
    EI = a["dn0"].shape[1]
    EG = 2 * EI
    EC = EI // 2
    SI = a["sdn0"].shape[0]
    SG = 2 * SI
    SCH = SG // P
    SFULL = SI // P
    SREM = SI - SFULL * P
    E = (a["gu0"].shape[0], a["gu1"].shape[0])
    TOPK = (2, 4)
    NG = tuple(((T * TOPK[l] + E[l] * (P - 1)) // P + 1) // 2 for l in range(2))
    NS = tuple(2 * n for n in NG)

    xs = [nc.dram_tensor(f"expert_in_{l}", [NS[l] * P, D], F32, kind="Internal").ap() for l in range(2)]
    ys = [nc.dram_tensor(f"expert_out_{l}", [NS[l] * P, D], F32, kind="Internal").ap() for l in range(2)]

    with ExitStack() as ctx:
        def sb(name, shape, dt=F32):
            return ctx.enter_context(nc.sbuf_tensor("sb_" + name, shape, dt))

        def sem(name):
            return ctx.enter_context(nc.semaphore(name))

        PS = ctx.enter_context(nc.psum_tensor("PS", [P, 8, 512], F32))

        x_sb = sb("x_sb", [P, NT, D])
        idf = sb("idf", [P, P])
        idh = sb("idh", [P, P], F16)
        ones_h = sb("ones_h", [P, P], F16)
        tri = sb("tri", [P, P], F16)
        headmask = sb("headmask", [P, P])
        lower = sb("lower", [P, 16, 16])
        tileno = sb("tileno", [1, max(NS)])
        swb = sb("swb", [P, 1])
        mhalf = sb("mhalf", [P, NT])
        zero = sb("zero", [P, D])

        wa0 = sb("wa0", [P, 2, C, 5 * D], F16)
        wa1 = sb("wa1", [P, 2, C, 4 * D], F16)
        rw = [sb(f"rw{l}", [P, 2, C, E[l] + 1], F16) for l in range(2)]
        ctxT = sb("ctxT_hl", [P, 2, C, CTX], F16)
        EXP_COLS = 16 * (2 * C * EG + 2 * 2 * D)
        region = sb("region", [P, EXP_COLS], F16)
        reg32 = region[:, :].bitcast(F32)
        half = EXP_COLS // 2
        GU = (region[:, half:half + 8 * 4 * EG // 1].rearrange("p (e h c n) -> p e h c n", e=8, h=2, c=C),
              region[:, 0:16 * 4 * EG].rearrange("p (e h c n) -> p e h c n", e=16, h=2, c=C))
        DN = (region[0:EC, half + 8 * 4 * EG:EXP_COLS].rearrange("p (e h c n) -> p e h c n", e=8, h=2, c=2),
              region[0:EC, 16 * 4 * EG:EXP_COLS].rearrange("p (e h c n) -> p e h c n", e=16, h=2, c=2))
        sgu = sb("sgu", [P, 2, C, SG], F16)
        sdn = sb("sdn", [P, 2, SFULL + 1, D], F16)
        stg = sb("stg", [P, 4, 2 * EG])

        xnT = sb("xnT", [P, 2, C, T], F16)
        KV = xnT[:, :, :, :].rearrange("p h c t -> p h (c t)").rearrange(
            "p h (b m k e) -> p h b m k e", b=NB, m=C, k=2)
        xnf = sb("xnf", [P, NT, D])
        Kpad = xnf[:, :, :].rearrange("p t d -> p (t d)").bitcast(F16).rearrange("p (h k) -> p h k", h=HEADS)
        Kg = Kpad.rearrange("p (g f) k -> p g f k", f=4)
        Vi = sb("Vi", [P, KT, D], F16)
        sv = sb("sv", [P, C])
        bq = sb("bq", [P, D])
        bk = sb("bk", [P, D])
        bp = sb("bp", [P, D])
        bv = sb("bv", [P, C])
        nmr = sb("nmr", [P, NT])
        g4 = sb("g4", [P, 4])
        tg = sb("tg", [P, 4])
        tgw = sb("tgw", [P, 4])
        mv = sb("mv", [P, NT, 2])
        bst = sb("bst", [P, 4, 6])
        mv1 = sb("mv1", [P, 2])
        ve = sb("ve", [P, NT])
        rstd = sb("rstd", [P, NT])
        wk1 = sb("wk1", [P, 4, 512])
        wkh = sb("wkh", [P, 8, 512], F16)
        w0_as_f32 = wa0[:, :, :, :].rearrange("p h c n -> p (h c n)").bitcast(F32)
        xg = w0_as_f32.rearrange("p (r d) -> p r d", d=D)
        xn32 = xnT[:, :, :, :].rearrange("p h c t -> p (h c t)").bitcast(F32)
        low32 = reg32[:, 6144:half // 2].rearrange("p (r n) -> p r n", n=512)
        lg = sb("lg", [P, NT, 17])
        bgh = lg[0:1, :, :].rearrange("p t e -> p (t e)")[:, 0:D].bitcast(F16).rearrange("p (h n) -> p h n", h=2)
        bg = reg32[0:1, 5700:5700 + D]
        ex = sb("ex", [P, NT, 16])
        order = sb("order", [P, 16])
        selm = sb("selm", [P, NT + 1, 16], F16)
        slotv = sb("slotv", [P, NT, 16])
        sm = sb("sm", [P, 16, 16])
        slotk = sb("slotk", [P, 4, NT])
        slotu = sb("slotu", [P, 4, NT], U32)
        wsel = sb("wsel", [P, 4, NT])
        sgate = sb("sgate", [P, NT])
        texp = sb("texp", [1, max(NS)], I32)
        texpf = sb("texpf", [1, max(NS)])

        phase = sem("phase")
        const_ready = sem("const_ready")
        ld_x = sem("ld_x"); ld_ctx = sem("ld_ctx"); ld_w0 = sem("ld_w0"); ld_w1 = sem("ld_w1")
        ld_small = sem("ld_small"); ld_rw = sem("ld_rw")
        hi_done = sem("hi_done"); lo_done = sem("lo_done")
        tg_ready = sem("tg_ready"); tgw_ready = sem("tgw_ready")
        stg_loaded = [sem(f"stg_loaded{i}") for i in range(4)]
        stg_split = [sem(f"stg_split{i}") for i in range(4)]
        shared_ready = [sem(f"shared_ready{l}") for l in range(2)]
        experts_ready = [sem(f"experts_ready{l}") for l in range(2)]
        shared_used = sem("shared_used"); experts_used = sem("experts_used")
        zeroed = [sem(f"zeroed{l}") for l in range(2)]
        stats_ready = sem("stats_ready"); rstd_ready = sem("rstd_ready")
        out_done = sem("out_done")

        block = ctx.enter_context(nc.Block())

        def steps(eng, total, unroll, lead, tail, fn):
            rounds = (total - lead - tail) // unroll
            for s in range(lead):
                fn(0, s)
            if rounds > 0:
                with eng.Fori(0, rounds) as i:
                    for s in range(unroll):
                        fn(i * unroll, lead + s)
            for s in range(lead + rounds * unroll, total):
                fn(0, s)

        def at_least(eng, s, base, n):
            if isinstance(base, int) and base + n <= 0:
                return
            assert isinstance(base, int) or n > 0, "a wait on a register's value has to be positive"
            if isinstance(s, Count):
                s, n = s.sem, n + s.start
            if isinstance(base, int):
                if base + n > 0:
                    eng.wait_ge(s, base + n)
            else:
                eng.wait_ge(s, base + n)

        def meet(eng, n):
            eng.drain().then_inc(phase, 1)
            eng.wait_ge(phase, 3 * n)

        w0f, w1f, ctxf = reg32[:, 0:2560], reg32[:, 2560:4608], reg32[:, 4608:5632]
        rwf = [reg32[:, 5632:5632 + C * 9], reg32[:, 5664:5664 + C * 17]]

        def inside(base, s, lo, hi):
            return not isinstance(base, int) or lo <= base + s < hi

        def bc(ap, n):
            return ap.unsqueeze(len(ap.shape)).broadcast_to(list(ap.shape) + [n])

        kv_ps = sem("kv_ps"); kv_parts = sem("kv_parts"); kv_k = sem("kv_k"); kv_kh = sem("kv_kh")
        kv_kl = sem("kv_kl"); sum_ps = sem("sum_ps"); sum_f = sem("sum_f"); sum_hi = sem("sum_hi")
        nm_ready = sem("nm_ready")
        a_xn = sem("a_xn"); a_xT = sem("a_xT"); a_xh = sem("a_xh"); a_xl = sem("a_xl"); a_qg = sem("a_qg")
        a_act = sem("a_act"); a_phi = sem("a_phi"); a_phih = sem("a_phih"); a_phil = sem("a_phil")
        a_nd = sem("a_nd"); a_og = sem("a_og"); a_ogT = sem("a_ogT"); a_ogh = sem("a_ogh")
        a_ogl = sem("a_ogl"); a_out = sem("a_out"); a_x = sem("a_x")
        la_e, la_r, la_phi, la_att, la_og = (low32[:, i] for i in range(5))
        la_t = (low32[:, 5], low32[:, 6])
        la_z = sm[:, 0:2, :]
        la_x = [(wkh[:, 2 * u], wkh[:, 2 * u + 1]) for u in range(2)]
        la_ph, la_pl, la_oh, la_ol = (wkh[:, 4 + i] for i in range(4))

        z_eps = sb("z_eps", [P, 1])

        def stats(*tiles):
            nc.vector.drain()
            for n, t in enumerate(tiles):
                nc.vector.bn_stats(bst[:, n, :], x_sb[:, t, :])
            nc.vector.drain()
            for n, t in enumerate(tiles):
                nc.vector.bn_aggr(mv[:, t, :], bst[:, n, :])

        def stats_end(n):
            nc.vector.drain()
            nc.vector.tensor_scalar(ve[:, :], mv[:, :, 1], LN_EPS, None, ALU.add).then_inc(stats_ready, 1)

        def mm3(out_, lhs, rhs, more=False, begun=False):
            for c in range(C):
                for n, (i, j) in enumerate(HL):
                    last = nc.tensor.matmul(out_, lhs(i, c), rhs(j, c), start=(c == 0 and n == 0 and not begun),
                                            stop=(c == C - 1 and n == 2 and not more))
            return last

        KSH = SFULL + 1
        BLK = T // 512

        def both(name, *first):
            s = sem(name)
            return Count(s, 0), Count(s, first[0])

        r_xn = both("r_xn", NT)
        r_xT = both("r_xT", NT)
        r_xh = both("r_xh", NT)
        r_xl = both("r_xl", NT)
        r_lg = both("r_lg", NT)
        r_lgc = both("r_lgc", NT)
        r_shift = both("r_shift", 1)
        r_exp = both("r_exp", 1)
        r_sel = both("r_sel", 1)
        r_count = both("r_count", 1)
        r_slots = both("r_slots", 1)
        s_gu = both("s_gu", BLK * KSH)
        s_silu = both("s_silu", BLK * KSH)
        s_h = both("s_h", BLK * KSH)
        s_hh = both("s_hh", BLK * KSH)
        s_hl = both("s_hl", BLK * KSH)
        s_d = both("s_d", BLK * KSH)
        s_accr = both("s_accr", BLK)
        e_xT = both("e_xT", NG[0])
        e_xh = both("e_xh", NG[0])
        e_xl = both("e_xl", NG[0])
        e_gu = both("e_gu", NG[0])
        e_silu = both("e_silu", NG[0])
        e_h = both("e_h", NG[0])
        e_hT = both("e_hT", NG[0])
        e_hh = both("e_hh", NG[0])
        e_hl = both("e_hl", NG[0])
        e_d = both("e_d", NG[0])
        e_y = both("e_y", NG[0])
        e_ld = list(zip(*(both(f"e_ld{u}", 16 * (NG[0] // 2)) for u in range(2))))
        e_st = list(zip(*(both(f"e_st{u}", 16 * (NG[0] // 2)) for u in range(2))))
        RING = (4, 2)
        c_ld = list(zip(*(both(f"c_ld{r}", 16 * TOPK[0] * NT // RING[0]) for r in range(RING[0]))))
        c_used = both("c_used", NT)
        scattered = both("scattered", 16 * NT * TOPK[0])

        def route_pe(pe, l):
            n = E[l] + 1
            for t in range(NT + 1):
                if t < NT:
                    at_least(pe, r_xn[l], 0, t + 1)
                    if t >= 2:
                        at_least(pe, r_xl[l], 0, t - 1)
                    for c in range(C):
                        last = nc.tensor.transpose(PS[:, t % 2, c * P:(c + 1) * P], xnf[:, t, c * P:(c + 1) * P], idf[:, :])
                    last.then_inc(r_xT[l].sem, 1)
                if t >= 1:
                    at_least(pe, r_xh[l], 0, t)
                    at_least(pe, r_xl[l], 0, t)
                    if t >= 3:
                        at_least(pe, r_lgc[l], 0, t - 2)
                    mm3(PS[:, 2 + (t - 1) % 2, 0:n], lambda i, c: xnT[:, i, c, (t - 1) * P:t * P],
                        lambda j, c: rw[l][:, j, c, :]).then_inc(r_lg[l].sem, 1)
            at_least(pe, r_sel[l], 0, 1)
            cnt = PS[:, 0, 0:(NT + 1) * E[l]]
            nc.tensor.matmul(cnt, tri[:, :], selm[:, :, 0:E[l]], start=True, stop=False, skip_group_check=True)
            for t in range(NT):
                last = nc.tensor.matmul(PS[:, 0, (t + 1) * E[l]:(NT + 1) * E[l]], ones_h[:, :],
                                        selm[:, t:t + 1, 0:E[l]].broadcast_to([P, NT - t, E[l]]),
                                        start=False, stop=(t == NT - 1), skip_group_check=True)
            last.then_inc(r_count[l].sem, 1)
            meet(pe, 3 + 4 * l)

        def route_act(act, l):
            for t in range(NT):
                at_least(act, r_xT[l], 0, t + 1)
                nc.scalar.activation(xnT[:, 0, :, t * P:(t + 1) * P],
                                     PS[:, t % 2, 0:D].rearrange("p (c n) -> p c n", c=C), ACT.Copy).then_inc(r_xh[l].sem, 1)
            at_least(act, r_shift[l], 0, 1)
            nc.scalar.activation(ex[:, :, 0:E[l]], ex[:, :, 0:E[l]], ACT.Exp)
            nc.scalar.activation(sm[:, 1, :], lg[:, :, E[l]], ACT.Exp, scale=-1.0).then_inc(r_exp[l].sem, 1)
            meet(act, 3 + 4 * l)

        def route_dve(dve, l):
            n, k_ = E[l], TOPK[l]
            dve.wait_ge(rstd_ready, 2 + 2 * l)
            for t in range(NT + 2):
                if t < NT:
                    nc.vector.tensor_scalar(xnf[:, t, :], x_sb[:, t, :], mv[:, t, 0:1], rstd[:, t:t + 1],
                                            ALU.subtract, ALU.mult).then_inc(r_xn[l].sem, 1)
                if 1 <= t <= NT:
                    at_least(dve, r_xh[l], 0, t)
                    s = slice((t - 1) * P, t * P)
                    nc.vector.tensor_tensor(xnT[:, 1, :, s], PS[:, (t - 1) % 2, 0:D].rearrange("p (c n) -> p c n", c=C),
                                            xnT[:, 0, :, s], ALU.subtract).then_inc(r_xl[l].sem, 1)
                if t >= 2:
                    at_least(dve, r_lg[l], 0, t - 1)
                    nc.vector.tensor_scalar(lg[:, t - 2, 0:n + 1], PS[:, 2 + t % 2, 0:n + 1], 1 / SW, None,
                                            ALU.mult).then_inc(r_lgc[l].sem, 1)
            dve.drain()
            L = lg[:, :, 0:n]
            flat = wk1[:, :, :].rearrange("p a b -> p (a b)")
            M = NT * n
            hot = flat[:, 0:k_ * M].rearrange("p (k t e) -> p k t e", k=k_, e=n)
            left = flat[:, 1024:1024 + M].rearrange("p (t e) -> p t e", e=n)
            tied = flat[:, 1536:1536 + M].rearrange("p (t e) -> p t e", e=n)
            prod = flat[:, 1024:1024 + k_ * M].rearrange("p (k t e) -> p k t e", k=k_, e=n)
            for k in range(k_):
                src = L if k == 0 else left
                nc.vector.tensor_reduce(sm[:, 0, :], src, AX, ALU.max)
                dve.drain()
                if k == 0:
                    nc.vector.tensor_tensor(ex[:, :, 0:n], L, bc(sm[:, 0, :], n), ALU.subtract).then_inc(r_shift[l].sem, 1)
                nc.vector.tensor_tensor(tied, src, bc(sm[:, 0, :], n), ALU.is_equal)
                dve.drain()
                nc.vector.tensor_tensor(tied, tied, order[:, 0:n].unsqueeze(1).broadcast_to([P, NT, n]), ALU.mult)
                dve.drain()
                nc.vector.tensor_reduce(sm[:, 8, :], tied, AX, ALU.max)
                dve.drain()
                nc.vector.tensor_tensor(hot[:, k], tied, bc(sm[:, 8, :], n), ALU.is_equal)
                dve.drain()
                nc.vector.scalar_tensor_tensor(left, hot[:, k], -3e38, src, ALU.mult, ALU.add)
                dve.drain()
            nc.vector.tensor_scalar(selm[:, 0:NT, 0:n], left, -1.5e38, None, ALU.is_lt).then_inc(r_sel[l].sem, 1)
            at_least(dve, r_exp[l], 0, 1)
            dve.drain()
            for k in range(k_):
                nc.vector.tensor_tensor(prod[:, k], hot[:, k], ex[:, :, 0:n], ALU.mult)
            dve.drain()
            nc.vector.tensor_reduce(wsel[:, 0:k_, :], prod, AX, ALU.add)
            dve.drain()
            if l == 0:
                nc.vector.tensor_tensor(sm[:, 2, :], wsel[:, 0, :], wsel[:, 1, :], ALU.add)
            else:
                nc.vector.tensor_reduce(sm[:, 2, :], ex[:, :, 0:n], AX, ALU.add)
            nc.vector.tensor_scalar(sm[:, 1, :], sm[:, 1, :], 1.0, None, ALU.add)
            dve.drain()
            nc.vector.reciprocal(sm[:, 2, :], sm[:, 2, :])
            nc.vector.reciprocal(sm[:, 1, :], sm[:, 1, :])
            dve.drain()
            for k in range(k_):
                nc.vector.scalar_tensor_tensor(wsel[:, k, :], wsel[:, k, :], tgw[:, 2 + l:3 + l], sm[:, 2, :],
                                               ALU.mult, ALU.mult)
            nc.vector.tensor_scalar(sgate[:, :], sm[:, 1, :], tgw[:, 2 + l:3 + l], None, ALU.mult)
            at_least(dve, r_count[l], 0, 1)
            nc.vector.tensor_scalar(sm[:, 3, 0:n], PS[:, 0, NT * n:(NT + 1) * n], 1 / P,
                                    (P - 1) / P - 0.5 + 0.5 / P, ALU.mult, ALU.add)
            dve.drain()
            nc.vector.tensor_scalar(sm[:, 3, 0:n], sm[:, 3, 0:n], MAGIC, -MAGIC, ALU.add, ALU.add)
            dve.drain()
            pre = flat[:, 1024:1024 + n * n].rearrange("p (e f) -> p e f", e=n)
            nc.vector.tensor_tensor(pre, sm[:, 3:4, 0:n].broadcast_to([P, n, n]), lower[:, 0:n, 0:n], ALU.mult)
            dve.drain()
            nc.vector.tensor_reduce(sm[:, 4, 0:n], pre, AX, ALU.add)
            dve.drain()
            nc.vector.tensor_tensor(sm[:, 5, 0:n], sm[:, 4, 0:n], sm[:, 3, 0:n], ALU.add)
            nc.vector.tensor_scalar(sm[:, 6, 0:n], sm[:, 4, 0:n], float(P), None, ALU.mult)
            dve.drain()
            nc.vector.tensor_tensor(slotv[:, :, 0:n], PS[:, 0, 0:NT * n].rearrange("p (t e) -> p t e", e=n),
                                    sm[:, 6:7, 0:n].broadcast_to([P, NT, n]), ALU.add)
            dve.drain()
            for k in range(k_):
                nc.vector.tensor_tensor(prod[:, k], hot[:, k], slotv[:, :, 0:n], ALU.mult)
            dve.drain()
            nc.vector.tensor_reduce(slotk[:, 0:k_, :], prod, AX, ALU.add)
            dve.drain()
            nc.vector.tensor_copy(slotu[:, 0:k_, :], slotk[:, 0:k_, :])
            w = flat[0:1, 0:NS[l] * n].rearrange("p (j e) -> p j e", e=n)
            nc.vector.tensor_tensor(w, bc(tileno[:, 0:NS[l]], n), sm[0:1, 5:6, 0:n].broadcast_to([1, NS[l], n]), ALU.is_ge)
            dve.drain()
            nc.vector.tensor_reduce(texpf[:, 0:NS[l]], w, AX, ALU.add)
            dve.drain()
            nc.vector.tensor_scalar(texp[:, 0:NS[l]], texpf[:, 0:NS[l]], float(n - 1), None, ALU.min)
            dve.drain().then_inc(r_slots[l].sem, 1)
            meet(dve, 3 + 4 * l)

        def group_rows(ap, base, s):
            v = ap.rearrange("(g n p) d -> g p n d", p=P, n=2)
            return v[base + s] if isinstance(base, int) else \
                v[bass.ds(base + s, 1), :, :, :].rearrange("o p n d -> (o p) n d")

        def ffn_dma(sp, l):
            at_least(sp, scattered[l], 0, 16 * NT * TOPK[l])

            def group(base, s):
                u = s % 2
                if inside(base, s, 0, NG[l]):
                    at_least(sp, e_xT[l], base, s - 1)
                    sp.dma_start(xg[:, 2 * u:2 * u + 2, :], group_rows(xs[l], base, s)).then_inc(e_ld[l][u].sem, 16)
                if inside(base, s, 4, NG[l] + 4):
                    at_least(sp, e_y[l], base, s - 3)
                    sp.dma_start(group_rows(ys[l], base, s - 4), xg[:, 4 + 2 * u:6 + 2 * u, :])\
                        .then_inc(e_st[l][u].sem, 16)
            steps(sp, NG[l] + 4, 2, 4, 4, group)

        def ffn_pool(pl, l):
            at_least(pl, r_slots[l], 0, 1)
            pl.wait_ge(zeroed[l], 16)
            for t in range(NT):
                for k in range(TOPK[l]):
                    nc.gpsimd.indirect_dma_start(xs[l][:, :], bass.IndirectOffsetOnAxis(ap=slotu[:, k, t:t + 1], axis=0),
                                                 xnf[:, t, :], None).then_inc(scattered[l].sem, 16)
            for u in range(2):
                at_least(pl, e_st[l][u], 0, 16 * (NG[l] // 2))
            for t in range(NT):
                r = t % RING[l]
                at_least(pl, c_used[l], 0, t + 1 - RING[l])
                for k in range(TOPK[l]):
                    nc.gpsimd.indirect_dma_start(xg[:, r * TOPK[l] + k, :], None, ys[l][:, :],
                                                 bass.IndirectOffsetOnAxis(ap=slotu[:, k, t:t + 1], axis=0))\
                        .then_inc(c_ld[l][r].sem, 16)

        HALF = BLK // 2 * KSH

        def halves(half, fn):
            for s in range(half * HALF, (half + 1) * HALF + 1):
                fn(s, s < (half + 1) * HALF, s > half * HALF)

        def ffn_pe(pe, l):
            def shared_step(s, front, back):
                u, k, b = s % 2, s % KSH, s // KSH
                if front:
                    at_least(pe, s_h[l], 0, s - 1)
                    for h in range(2 if k < SFULL else 1):
                        last = mm3(PS[:, 2 * u + h, :], lambda i, c: sgu[:, i, c, (2 * k + h) * P:(2 * k + h + 1) * P],
                                   lambda j, c: xnT[:, j, c, b * 512:(b + 1) * 512])
                    last.then_inc(s_gu[l].sem, 1)
                if back:
                    kd, v = (s - 1) % KSH, (s - 1) % 2
                    r = P if kd < SFULL else SREM
                    at_least(pe, s_hh[l], 0, s)
                    at_least(pe, s_hl[l], 0, s)
                    if kd == 0:
                        at_least(pe, s_accr[l], 0, (s - 1) // KSH)
                    for i in range(4):
                        for n, (h, j) in enumerate(HL):
                            last = nc.tensor.matmul(PS[:, 4 + i, 0:D], wkh[0:r, 2 * h + v, i * P:(i + 1) * P],
                                                    sdn[0:r, j, kd, :], start=(kd == 0 and n == 0),
                                                    stop=(kd == KSH - 1 and n == 2))
                    last.then_inc(s_d[l].sem, 1)
            pe.wait_ge(shared_ready[l], 1)
            halves(0, shared_step)

            pe.wait_ge(experts_ready[l], 1)
            at_least(pe, r_slots[l], 0, 1)
            at_least(pe, s_accr[l], 0, BLK // 2)

            def transposes(base, s):
                at_least(pe, e_ld[l][s % 2], base * 8, 16 * (s // 2 + 1))
                for n in range(2):
                    for c in range(C):
                        last = nc.tensor.transpose(PS[:, 4 + s % 2, (2 * n + c) * P:(2 * n + c + 1) * P],
                                                   xg[:, 2 * (s % 2) + n, c * P:(c + 1) * P], idf[:, :])
                last.then_inc(e_xT[l].sem, 1)

            def experts(base, s):
                j = slice(2 * (base + s), 2 * (base + s) + 2) if isinstance(base, int) else bass.ds(base * 2 + 2 * s, 2)
                return nc.values_load_multi_w_load_instructions(
                    texp[0:1, j], [mybir.EngineType.PE], min_val=0, max_val=E[l] - 1,
                    skip_runtime_bounds_check_because="the table's entries are clamped to E - 1 where it is written")[1]

            def group(base, s):
                u = s % 2
                if inside(base, s, 0, NG[l] - 1):
                    transposes(base, s + 1)
                if inside(base, s, 0, NG[l]):
                    e = experts(base, s)
                    at_least(pe, e_xl[l], base, s + 1)
                    for n in range(2):
                        last = mm3(PS[:, 2 * u + n, 0:EG], lambda i, c: wkh[:, 2 * u + i, (2 * n + c) * P:(2 * n + c + 1) * P],
                                   lambda h, c: GU[l][:, bass.ds(e[n], 1), h, c, :].rearrange("p o n -> p (o n)"))
                    last.then_inc(e_gu[l].sem, 1)
                at_least(pe, e_hl[l], base, s - 1)
                if inside(base, s, 1, NG[l] + 1):
                    at_least(pe, e_h[l], base, s)
                    for n in range(2):
                        for c in range(C):
                            last = nc.tensor.transpose(PS[0:EC, 6, (2 * n + c) * P:(2 * n + c + 1) * P],
                                                       wk1[:, 3 - u, n * EI + c * EC:n * EI + (c + 1) * EC], idf[:, :])
                    last.then_inc(e_hT[l].sem, 1)
                if inside(base, s, 2, NG[l] + 2):
                    e = experts(base, s - 2)
                    at_least(pe, e_y[l], base, s - 2)
                    for n in range(2):
                        last = mm3(PS[:, 7, n * D:(n + 1) * D],
                                   lambda i, c: wkh[0:EC, 4 + 2 * u + i, (2 * n + c) * P:(2 * n + c + 1) * P],
                                   lambda h, c: DN[l][:, bass.ds(e[n], 1), h, c, :].rearrange("p o n -> p (o n)"))
                    last.then_inc(e_d[l].sem, 1)
            transposes(0, 0)
            steps(pe, NG[l] + 2, 2, 4, 3, group)
            pe.drain().then_inc(experts_used, 1)
            at_least(pe, e_y[l], 0, NG[l])
            halves(1, shared_step)
            pe.drain().then_inc(shared_used, 1)
            meet(pe, 4 + 4 * l)

        def ffn_act(act, l):
            def shared_step(s, front, back):
                if front:
                    u, k = s % 2, s % KSH
                    r = P if k < SFULL else SREM
                    at_least(act, s_gu[l], 0, s + 1)
                    at_least(act, s_h[l], 0, s - 1)
                    nc.scalar.activation(wk1[0:r, u, :], PS[0:r, 2 * u, :], ACT.Silu, scale=1 / SW).then_inc(s_silu[l].sem, 1)
                    at_least(act, s_h[l], 0, s + 1)
                    at_least(act, s_d[l], 0, s - 1)
                    nc.scalar.activation(wkh[0:r, u, :], wk1[0:r, 2 + u, :], ACT.Copy).then_inc(s_hh[l].sem, 1)
            halves(0, shared_step)

            def high_x(base, s):
                at_least(act, e_xT[l], base, s + 1)
                nc.scalar.activation(wkh[:, 2 * (s % 2), :], PS[:, 4 + s % 2, :], ACT.Copy).then_inc(e_xh[l].sem, 1)

            def group(base, s):
                u = s % 2
                if inside(base, s, 0, NG[l] - 1):
                    high_x(base, s + 1)
                if inside(base, s, 0, NG[l]):
                    at_least(act, e_gu[l], base, s + 1)
                    at_least(act, e_h[l], base, s - 1)
                    nc.scalar.activation(wk1[:, u, 0:EG].rearrange("p (n i) -> p n i", n=2), PS[:, 2 * u:2 * u + 2, 0:EI],
                                         ACT.Silu, scale=1 / SW).then_inc(e_silu[l].sem, 1)
                if inside(base, s, 1, NG[l] + 1):
                    at_least(act, e_hT[l], base, s)
                    nc.scalar.activation(wkh[0:EC, 6 - 2 * u, :], PS[0:EC, 6, :], ACT.Copy).then_inc(e_hh[l].sem, 1)
            high_x(0, 0)
            steps(act, NG[l] + 1, 2, 4, 2, group)
            halves(1, shared_step)
            meet(act, 4 + 4 * l)

        def ffn_dve(dve, l):
            def shared_out(b):
                at_least(dve, s_d[l], 0, (b + 1) * KSH)
                for i in range(4):
                    t = 4 * b + i
                    last = nc.vector.scalar_tensor_tensor(x_sb[:, t, :], PS[:, 4 + i, 0:D], sgate[:, t:t + 1], x_sb[:, t, :],
                                                          ALU.mult, ALU.add)
                last.then_inc(s_accr[l].sem, 1)

            def combine(t):
                r = t % RING[l]
                at_least(dve, c_ld[l][r], 0, 16 * TOPK[l] * (t // RING[l] + 1))
                for k in range(TOPK[l]):
                    dve.drain()
                    last = nc.vector.scalar_tensor_tensor(x_sb[:, t, :], xg[:, r * TOPK[l] + k, :], wsel[:, k, t:t + 1],
                                                          x_sb[:, t, :], ALU.mult, ALU.add)
                last.then_inc(c_used[l].sem, 1)
                if l == 0:
                    stats(t)

            def shared_step(s, front, back):
                u, k, b = s % 2, s % KSH, s // KSH
                if front:
                    r = P if k < SFULL else SREM
                    at_least(dve, s_silu[l], 0, s + 1)
                    at_least(dve, s_hh[l], 0, s - 1)
                    up = PS[0:r, 2 * u + 1, :] if k < SFULL else PS[SREM:2 * SREM, 2 * u, :]
                    nc.vector.scalar_tensor_tensor(wk1[0:r, 2 + u, :], up, 1 / SW, wk1[0:r, u, :],
                                                   ALU.mult, ALU.mult).then_inc(s_h[l].sem, 1)
                    at_least(dve, s_hh[l], 0, s + 1)
                    at_least(dve, s_d[l], 0, s - 1)
                    nc.vector.tensor_tensor(wkh[0:r, 2 + u, :], wk1[0:r, 2 + u, :], wkh[0:r, u, :],
                                            ALU.subtract).then_inc(s_hl[l].sem, 1)
                if back and k == 0:
                    shared_out(b - 1)
                if front and s >= HALF + 1:
                    combine(s - HALF - 1)
            halves(0, shared_step)

            def low_x(base, s):
                at_least(dve, e_xh[l], base, s + 1)
                nc.vector.tensor_tensor(wkh[:, 2 * (s % 2) + 1, :], PS[:, 4 + s % 2, :], wkh[:, 2 * (s % 2), :],
                                        ALU.subtract).then_inc(e_xl[l].sem, 1)

            def group(base, s):
                u = s % 2
                if inside(base, s, 0, NG[l] - 1):
                    low_x(base, s + 1)
                if inside(base, s, 0, NG[l]):
                    at_least(dve, e_silu[l], base, s + 1)
                    nc.vector.scalar_tensor_tensor(wk1[:, 2 + u, 0:EG].rearrange("p (n i) -> p n i", n=2),
                                                   PS[:, 2 * u:2 * u + 2, EI:EG], 1 / SW,
                                                   wk1[:, u, 0:EG].rearrange("p (n i) -> p n i", n=2),
                                                   ALU.mult, ALU.mult).then_inc(e_h[l].sem, 1)
                if inside(base, s, 1, NG[l] + 1):
                    at_least(dve, e_hh[l], base, s)
                    nc.vector.tensor_tensor(wkh[0:EC, 7 - 2 * u, :], PS[0:EC, 6, :], wkh[0:EC, 6 - 2 * u, :],
                                            ALU.subtract).then_inc(e_hl[l].sem, 1)
                if inside(base, s, 2, NG[l] + 2):
                    at_least(dve, e_d[l], base, s - 1)
                    at_least(dve, e_st[l][u], base * 8, 16 * ((s - 2) // 2))
                    nc.vector.tensor_copy(xg[:, 4 + 2 * u:6 + 2 * u, :].rearrange("p n d -> p (n d)"), PS[:, 7, :])\
                        .then_inc(e_y[l].sem, 1)
            low_x(0, 0)
            steps(dve, NG[l] + 2, 2, 4, 3, group)
            halves(1, shared_step)
            for t in range(HALF - 1, NT):
                combine(t)
            if l == 0:
                stats_end(2)
            meet(dve, 4 + 4 * l)

        p_v = sem("p_v"); p_vq = sem("p_vq"); p_vT = sem("p_vT"); p_vd = sem("p_vd"); p_k = sem("p_k")
        p_kq = sem("p_kq"); p_kT = sem("p_kT"); p_kd = sem("p_kd"); p_zero = sem("p_zero")
        q_xn = sem("q_xn"); q_xT = sem("q_xT"); q_xh = sem("q_xh"); q_xl = sem("q_xl"); q_ps = sem("q_ps")
        q_int = sem("q_int"); q_T = sem("q_T"); q_ready = sem("q_ready")
        h_qk = sem("h_qk"); h_max = sem("h_max"); h_exp = sem("h_exp"); h_int = sem("h_int"); h_pT = sem("h_pT")
        h_pc = sem("h_pc"); h_pv = sem("h_pv")
        o_norm = sem("o_norm"); o_T = sem("o_T"); o_hi = sem("o_hi"); o_lo = sem("o_lo"); o_y = sem("o_y"); o_x = sem("o_x")
        PAIRS = HEADS // 2
        NQ = NT * PAIRS
        q_row = xn32[:, 0:D]
        q_f = xn32[:, D:2 * D]
        q_t = xn32[:, 2 * D:3 * D]
        o_n = xn32[:, 3 * D:4 * D]
        q_hl = xn32[:, 4 * D:5 * D].bitcast(F16).rearrange("p (h n) -> p h n", h=2)
        o_hl = xn32[:, 5 * D:6 * D].bitcast(F16).rearrange("p (h n) -> p h n", h=2)
        q_i = xn32[:, 6 * D:7 * D].bitcast(F16)
        q_iT = [xn32[:, (7 + u) * D:(8 + u) * D].bitcast(F16).rearrange("p (g n) -> p g n", g=4) for u in range(2)]
        small = xn32[:, 9 * D:10 * D].rearrange("p (a h) -> p a h", h=HEADS)
        q_s = [small[:, 2 + u] for u in range(2)]
        q_ns = [small[:, 4 + u] for u in range(2)]
        o_sum = [small[:, 6 + u] for u in range(2)]
        h_mx = [small[:, 8 + u, 0:2] for u in range(2)]
        h_nb = [small[:, 10 + u, 0:2] for u in range(2)]
        h_e = [wk1[:, 2 * u:2 * u + 2] for u in range(2)]
        h_p = [wkh[:, 2 * u:2 * u + 2] for u in range(2)]
        h_T = [wkh[:, 4 + 2 * u:6 + 2 * u] for u in range(2)]

        def attn1_keys_pe(pe):
            for m in range(C):
                last = mm3(PS[:, 6 + m, :], lambda i, c: wa1[:, i, c, 2 * D + m * P:2 * D + (m + 1) * P],
                           lambda j, c: ctxT[:, j, c, :])
            last.then_inc(p_v, 1)
            for t in range(KT):
                mm3(PS[:, t, 0:D], lambda i, c: ctxT[:, i, c, t * P:(t + 1) * P],
                    lambda j, c: wa1[:, j, c, D:2 * D]).then_inc(p_k, 1)
            pe.wait_ge(p_vq, 1)
            for m in range(C):
                for t in range(KT):
                    last = nc.tensor.transpose(PS[:, 6 + m, :].bitcast(F16)[:, t * P:(t + 1) * P],
                                               wkh[:, m, t * P:(t + 1) * P], idh[:, :])
            last.then_inc(p_vT, 1)
            for t in range(KT):
                pe.wait_ge(p_kq, t + 1)
                if t >= 2:
                    pe.wait_ge(p_kd, t - 1)
                for g in range(4):
                    last = nc.tensor.transpose(PS[:, 4 + t % 2, :].bitcast(F16)[:, g * P:(g + 1) * P],
                                               wkh[:, 4 + t, g * P:(g + 1) * P], idh[:, :])
                last.then_inc(p_kT, 1)

        def attn1_keys_act(act):
            act.wait_ge(p_vT, 1)
            for m in range(C):
                last = nc.scalar.activation(Vi[:, :, m * P:(m + 1) * P],
                                            PS[:, 6 + m, :].bitcast(F16)[:, 0:CTX].rearrange("p (t n) -> p t n", n=P),
                                            ACT.Copy)
            last.then_inc(p_vd, 1)
            act.wait_ge(p_zero, 1)
            for t in range(KT):
                act.wait_ge(p_kT, t + 1)
                for f in range(4):
                    r = slice(32 * f, 32 * (f + 1))
                    last = nc.scalar.activation(Kg[r, :, f, t * P:(t + 1) * P],
                                                PS[r, 4 + t % 2, :].bitcast(F16)[:, 0:4 * P].rearrange("p (g n) -> p g n", n=P),
                                                ACT.Copy)
                last.then_inc(p_kd, 1)

        def quantise(dve, x_, y_, s_, r_, n, scale=1.0):
            xg_ = x_.rearrange("p (h d) -> p h d", d=HD)
            nc.vector.tensor_reduce(s_, xg_, AX, ALU.max, apply_absolute_value=True)
            dve.drain()
            nc.vector.tensor_scalar(s_, s_, scale / 127.0, 1e-8, ALU.mult, ALU.max)
            dve.drain()
            nc.vector.reciprocal(r_, s_)
            dve.drain()
            if scale != 1.0:
                nc.vector.tensor_scalar(r_, r_, scale, None, ALU.mult)
                dve.drain()
            nc.vector.tensor_tensor(y_.rearrange("p (h d) -> p h d", d=HD), xg_, bc(r_, HD), ALU.mult)
            dve.drain()

        def attn1_keys_dve(dve):
            nc.vector.memset(Kpad.bitcast(U32), 0).then_inc(p_zero, 1)
            dve.wait_ge(p_v, 1)
            for m in range(C):
                nc.vector.tensor_scalar(wk1[:, m, :], PS[:, 6 + m, :], 1 / SW, bv[:, m:m + 1], ALU.mult, ALU.add)
                dve.drain()
                nc.vector.tensor_reduce(sv[:, m:m + 1], wk1[:, m, :], AX, ALU.max, apply_absolute_value=True)
            dve.drain()
            nc.vector.tensor_scalar(sv[:, :], sv[:, :], 1 / 127.0, 1e-8, ALU.mult, ALU.max)
            dve.drain()
            nc.vector.reciprocal(sm[:, 7, 0:C], sv[:, :])
            dve.drain()
            for m in range(C):
                nc.vector.tensor_scalar(wk1[:, m, :], wk1[:, m, :], sm[:, 7, m:m + 1], MAGIC, ALU.mult, ALU.add)
                dve.drain()
                last = nc.vector.tensor_scalar(wkh[:, m, :], wk1[:, m, :], -MAGIC, None, ALU.add)
            last.then_inc(p_vq, 1)
            for t in range(KT):
                dve.wait_ge(p_k, t + 1)
                kf, ki = wk1[:, 2 + t % 2, 0:D], wk1[:, 2 + t % 2, D:2 * D]
                dve.drain()
                nc.vector.scalar_tensor_tensor(kf, PS[:, t, 0:D], 1 / SW, bk[:, :], ALU.mult, ALU.add)
                dve.drain()
                quantise(dve, kf, ki, sm[:, 8, :], sm[:, 9, :], HEADS)
                nc.vector.tensor_scalar(ki, ki, MAGIC, -MAGIC, ALU.add, ALU.add)
                dve.drain()
                k3 = ki.rearrange("p (h d) -> p h d", d=HD)
                nc.vector.tensor_tensor(k3, k3, bc(sm[:, 8, :], HD), ALU.mult)
                dve.drain()
                kk = wkh[:, 4 + t, :].rearrange("p (h i d) -> p h i d", i=2, d=HD)
                nc.vector.tensor_copy(kk[:, :, 0, :], k3)
                dve.drain()
                nc.vector.tensor_tensor(kk[:, :, 1, :], k3, kk[:, :, 0, :], ALU.subtract).then_inc(p_kq, 1)

        def row_of(base, s, ap):
            if isinstance(base, int):
                return ap[:, base + s]
            v = ap[:, bass.ds(base + s, 1)]
            return v if len(ap.shape) == 2 else v.rearrange("p o d -> p (o d)")

        def attn1_pe(pe):
            attn1_keys_pe(pe)
            meet(pe, 5)

            def queries(tb, ts):
                at_least(pe, q_xn, tb, ts + 1)
                at_least(pe, o_x, tb, ts - 2)
                for c in range(C):
                    last = nc.tensor.transpose(PS[:, 7, c * P:(c + 1) * P], q_row[:, c * P:(c + 1) * P], idf[:, :])
                last.then_inc(q_xT, 1)

            def query_products(tb, ts):
                at_least(pe, q_xl, tb, ts + 1)
                mm3(PS[:, 7, 0:D], lambda i, c: q_hl[:, i, c * P:(c + 1) * P],
                    lambda j, c: wa1[:, j, c, 0:D]).then_inc(q_ps, 1)

            def query_transposes(tb, ts):
                at_least(pe, q_int, tb, ts + 1)
                for g in range(4):
                    last = nc.tensor.transpose(PS[:, 7, :].bitcast(F16)[:, g * P:(g + 1) * P],
                                               q_i[:, g * P:(g + 1) * P], idh[:, :])
                last.then_inc(q_T, 1)

            def logits(base, s):
                tb, ts, pair, u = base, s // PAIRS, s % PAIRS, s % 2
                b8 = base * PAIRS
                if pair == 0:
                    at_least(pe, q_ready, tb, ts + 1)
                at_least(pe, h_exp, b8, s - 1)
                at_least(pe, h_max, b8, s - 1)
                for h in range(2):
                    head = 2 * pair + h
                    last = nc.tensor.matmul(PS[:, 2 * u + h, :], q_iT[ts % 2][:, head // 4, :], Kpad[:, head, :],
                                            start=True, stop=True)
                last.then_inc(h_qk, 1)

            def values(base, s):
                b8, u = base * PAIRS, s % 2
                at_least(pe, h_int, b8, s + 1)
                at_least(pe, h_pc, b8, s - 1)
                bank = PS[:, 4 + u, :].bitcast(F16)
                for h in range(2):
                    for k in range(KT):
                        last = nc.tensor.transpose(bank[:, (h * KT + k) * P:(h * KT + k + 1) * P],
                                                   h_p[u][:, h, k * P:(k + 1) * P], idh[:, :])
                last.then_inc(h_pT, 1)

            def weighted(base, s):
                b8, u, pair = base * PAIRS, s % 2, s % PAIRS
                at_least(pe, h_pc, b8, s + 1)
                if pair == 0:
                    at_least(pe, o_norm, base, s // PAIRS)
                pt = h_T[u].rearrange("p a b -> p (a b)")
                for h in range(2):
                    head = 2 * pair + h
                    for k in range(KT):
                        last = nc.tensor.matmul(PS[:, 6, D + head * HD:D + (head + 1) * HD],
                                                pt[:, (h * KT + k) * P:(h * KT + k + 1) * P],
                                                Vi[:, k, head * HD:(head + 1) * HD], start=(k == 0), stop=(k == KT - 1))
                last.then_inc(h_pv, 1)

            def output_transposes(tb, ts):
                at_least(pe, o_norm, tb, ts + 1)
                at_least(pe, q_ready, tb, min(ts + 3, NT - tb) if isinstance(tb, int) else ts + 3)
                for c in range(C):
                    last = nc.tensor.transpose(PS[:, 7, c * P:(c + 1) * P], o_n[:, c * P:(c + 1) * P], idf[:, :])
                last.then_inc(o_T, 1)

            def project(tb, ts):
                at_least(pe, o_hi, tb, ts + 1)
                at_least(pe, o_lo, tb, ts + 1)
                mm3(PS[:, 7, 0:D], lambda i, c: o_hl[:, i, c * P:(c + 1) * P],
                    lambda j, c: wa1[:, j, c, 3 * D:4 * D]).then_inc(o_y, 1)

            def step(base, s):
                ts, pair = s // PAIRS, s % PAIRS
                if inside(base * PAIRS, s, 0, NQ - 1):
                    logits(base, s + 1)
                if inside(base * PAIRS, s, 1, NQ + 1):
                    values(base, s - 1)
                if inside(base * PAIRS, s, 2, NQ + 2):
                    weighted(base, s - 2)
                if inside(base, ts, 0, NT - 1):
                    if pair == 1:
                        queries(base, ts + 1)
                    if pair == 3:
                        query_products(base, ts + 1)
                    if pair == 5:
                        query_transposes(base, ts + 1)
                if inside(base, ts, 1, NT + 1):
                    if pair == 6:
                        output_transposes(base, ts - 1)
                    if pair == 7:
                        project(base, ts - 1)
            queries(0, 0)
            query_products(0, 0)
            query_transposes(0, 0)
            logits(0, 0)
            tiles(pe, step)
            meet(pe, 6)

        def tiles(eng, step):
            for s in range(2 * PAIRS):
                step(0, s)
            n = (NT - 3) // 2
            with eng.Fori(0, n) as i:
                for s in range(2 * PAIRS, 4 * PAIRS):
                    step(i * 2, s)
            for s in range(2 * PAIRS, (NT - 2 * n + 1) * PAIRS + 1):
                step(2 * n, s)

        def attn1_act(act):
            attn1_keys_act(act)
            meet(act, 5)

            def queries(tb, ts):
                at_least(act, q_xT, tb, ts + 1)
                at_least(act, q_ps, tb, ts)
                nc.scalar.activation(q_hl[:, 0, :], PS[:, 7, 0:D], ACT.Copy).then_inc(q_xh, 1)

            def query_copies(tb, ts):
                at_least(act, q_T, tb, ts + 1)
                nc.scalar.activation(q_iT[ts % 2].rearrange("p g n -> p (g n)"), PS[:, 7, :].bitcast(F16)[:, 0:2 * D],
                                     ACT.Copy).then_inc(q_ready, 1)

            def exponentials(base, s):
                b8, u, pair = base * PAIRS, s % 2, s % PAIRS
                v = (s // PAIRS) % 2
                at_least(act, h_max, b8, s + 1)
                at_least(act, h_int, b8, s - 1)
                for h in range(2):
                    head = 2 * pair + h
                    last = nc.scalar.activation(h_e[u][:, h, :], PS[:, 2 * u + h, :], ACT.Exp, bias=h_nb[u][:, h:h + 1],
                                                scale=q_s[v][:, head:head + 1], accum_out=o_sum[v][:, head:head + 1])
                last.then_inc(h_exp, 1)

            def copies(base, s):
                b8, u = base * PAIRS, s % 2
                at_least(act, h_pT, b8, s + 1)
                at_least(act, h_pv, b8, s - 1)
                nc.scalar.activation(h_T[u].rearrange("p a b -> p (a b)"), PS[:, 4 + u, :].bitcast(F16),
                                     ACT.Copy).then_inc(h_pc, 1)

            def output_high(tb, ts):
                at_least(act, o_T, tb, ts + 1)
                at_least(act, o_y, tb, ts)
                for c in range(C):
                    last = nc.scalar.activation(o_hl[:, 0, c * P:(c + 1) * P], PS[:, 7, c * P:(c + 1) * P], ACT.Copy,
                                                scale=sv[:, c:c + 1])
                last.then_inc(o_hi, 1)

            def step(base, s):
                ts, pair = s // PAIRS, s % PAIRS
                if inside(base * PAIRS, s, 0, NQ):
                    exponentials(base, s)
                if inside(base * PAIRS, s, 1, NQ + 1):
                    copies(base, s - 1)
                if inside(base, ts, 0, NT - 1):
                    if pair == 1:
                        queries(base, ts + 1)
                    if pair == 5:
                        query_copies(base, ts + 1)
                if inside(base, ts, 1, NT + 1) and pair == 6:
                    output_high(base, ts - 1)
            queries(0, 0)
            query_copies(0, 0)
            tiles(act, step)
            meet(act, 6)

        def attn1_dve(dve):
            attn1_keys_dve(dve)
            meet(dve, 5)
            dve.wait_ge(rstd_ready, 3)

            def queries(tb, ts):
                at_least(dve, q_xT, tb, ts)
                nc.vector.tensor_scalar(q_row, row_of(tb, ts, x_sb), row_of(tb, ts, mv)[:, 0:1],
                                        row_of(tb, ts, rstd)[:, 0:1] if not isinstance(tb, int) else rstd[:, tb + ts:tb + ts + 1],
                                        ALU.subtract, ALU.mult).then_inc(q_xn, 1)

            def queries_low(tb, ts):
                at_least(dve, q_xh, tb, ts + 1)
                at_least(dve, q_ps, tb, ts)
                nc.vector.tensor_tensor(q_hl[:, 1, :], PS[:, 7, 0:D], q_hl[:, 0, :], ALU.subtract).then_inc(q_xl, 1)

            def query_integers(tb, ts):
                v = ts % 2
                at_least(dve, q_ps, tb, ts + 1)
                nc.vector.scalar_tensor_tensor(q_f, PS[:, 7, 0:D], 1 / SW, bq[:, :], ALU.mult, ALU.add)
                dve.drain()
                at_least(dve, h_exp, tb * PAIRS, (ts - 1) * PAIRS)
                quantise(dve, q_f, q_t, q_s[v], small[:, 0], HEADS, 0.25)
                nc.vector.tensor_scalar(q_ns[v], q_s[v], -1.0, None, ALU.mult)
                at_least(dve, q_T, tb, ts)
                nc.vector.tensor_scalar(q_i.rearrange("p (h i d) -> p h i d", i=2, d=HD),
                                        q_t.rearrange("p (h d) -> p h d", d=HD).unsqueeze(2).broadcast_to([P, HEADS, 2, HD]),
                                        MAGIC, -MAGIC, ALU.add, ALU.add).then_inc(q_int, 1)

            def maxima(base, s):
                b8, u, pair = base * PAIRS, s % 2, s % PAIRS
                v = (s // PAIRS) % 2
                at_least(dve, h_qk, b8, s + 1)
                at_least(dve, h_exp, b8, s - 1)
                nc.vector.tensor_reduce(h_mx[u], PS[:, 2 * u:2 * u + 2, :], AX, ALU.max)
                dve.drain()
                for h in range(2):
                    last = nc.vector.tensor_scalar(h_nb[u][:, h:h + 1], h_mx[u][:, h:h + 1],
                                                   q_ns[v][:, 2 * pair + h:2 * pair + h + 1], LN255, ALU.mult, ALU.add)
                last.then_inc(h_max, 1)

            def integers(base, s):
                b8, u = base * PAIRS, s % 2
                at_least(dve, h_exp, b8, s + 1)
                at_least(dve, h_pT, b8, s - 1)
                nc.vector.tensor_scalar(h_p[u], h_e[u], MAGIC, -MAGIC, ALU.add, ALU.add).then_inc(h_int, 1)

            def normalised(tb, ts):
                v = ts % 2
                at_least(dve, h_pv, tb * PAIRS, (ts + 1) * PAIRS)
                at_least(dve, o_T, tb, ts)
                nc.vector.reciprocal(small[:, 1], o_sum[v])
                dve.drain()
                nc.vector.tensor_tensor(o_n.rearrange("p (h d) -> p h d", d=HD),
                                        PS[:, 6, D:2 * D].rearrange("p (h d) -> p h d", d=HD), bc(small[:, 1], HD),
                                        ALU.mult).then_inc(o_norm, 1)

            def output_low(tb, ts):
                at_least(dve, o_hi, tb, ts + 1)
                at_least(dve, o_y, tb, ts)
                for c in range(C):
                    last = nc.vector.scalar_tensor_tensor(o_hl[:, 1, c * P:(c + 1) * P], PS[:, 7, c * P:(c + 1) * P],
                                                          sv[:, c:c + 1], o_hl[:, 0, c * P:(c + 1) * P],
                                                          ALU.mult, ALU.subtract)
                last.then_inc(o_lo, 1)

            def update(tb, ts):
                at_least(dve, o_y, tb, ts + 1)
                xt = row_of(tb, ts, x_sb)
                nc.vector.scalar_tensor_tensor(xt, PS[:, 7, 0:D], tgw[:, 1:2], xt, ALU.mult, ALU.add)
                dve.drain()
                nc.vector.tensor_tensor(xt, xt, bp[:, :], ALU.add).then_inc(o_x, 1)
                dve.drain()
                nc.vector.bn_stats(bst[:, 0, :], xt)
                dve.drain()
                nc.vector.bn_aggr(mv1[:, :], bst[:, 0, :])
                dve.drain()
                nc.vector.tensor_copy(row_of(tb, ts, mv), mv1[:, :])

            def step(base, s):
                ts, pair = s // PAIRS, s % PAIRS
                if inside(base * PAIRS, s, 0, NQ):
                    maxima(base, s)
                if inside(base * PAIRS, s, 1, NQ + 1):
                    integers(base, s - 1)
                if inside(base, ts, 1, NT + 1):
                    if pair == 2:
                        normalised(base, ts - 1)
                    if pair == 7:
                        output_low(base, ts - 1)
                if inside(base, ts, 2, NT + 2) and pair == 0:
                    update(base, ts - 2)
                if inside(base, ts, 0, NT - 1):
                    if pair == 0:
                        queries(base, ts + 1)
                    if pair == 2:
                        queries_low(base, ts + 1)
                    if pair == 4:
                        query_integers(base, ts + 1)
            queries(0, 0)
            queries_low(0, 0)
            query_integers(0, 0)
            tiles(dve, step)
            stats_end(3)
            meet(dve, 6)

        @block.sync
        def _(sp):
            sp.dma_start(ctxf.rearrange("p (c n) -> p c n", c=C),
                         a["ctxT"].rearrange("(c p) n -> p c n", c=C)).then_inc(ld_ctx, 16)
            sp.dma_start(w0f.rearrange("p (c n) -> p c n", c=C),
                         a["wa0"].rearrange("(c p) n -> p c n", c=C)).then_inc(ld_w0, 16)
            sp.dma_start(x_sb[:, :, :], a["x"].rearrange("(t p) d -> p t d", p=P)).then_inc(ld_x, 16)
            sp.dma_start(g4[:, 0:2], a["g_xattn"].rearrange("(o n) -> o n", o=1).broadcast_to([P, 2])).then_inc(ld_small, 16)
            sp.dma_start(g4[:, 2:4], a["g_ffn"].rearrange("(o n) -> o n", o=1).broadcast_to([P, 2])).then_inc(ld_small, 16)
            for dst, name in ((bq, "bq"), (bk, "bk"), (bp, "bp")):
                sp.dma_start(dst[:, :], a[name].rearrange("(o n) -> o n", o=1).broadcast_to([P, D])).then_inc(ld_small, 16)
            sp.dma_start(bv[:, :], a["bvT"]).then_inc(ld_small, 16)
            sp.dma_start(bg[:, :], a["bg"].rearrange("(o n) -> o n", o=1)).then_inc(ld_small, 16)
            sp.dma_start(w1f.rearrange("p (c n) -> p c n", c=C),
                         a["wa1"].rearrange("(c p) n -> p c n", c=C)).then_inc(ld_w1, 16)
            for l in range(2):
                sp.dma_start(rwf[l].rearrange("p (c n) -> p c n", c=C),
                             a[f"rw{l}"].rearrange("(c p) n -> p c n", c=C)).then_inc(ld_rw, 16)
            if stage >= 3:
                sp.wait_ge(const_ready, 1)
                for l in range(2):
                    v = xs[l].rearrange("(p r) d -> p r d", p=P)
                    sp.dma_start(v, zero[:, :].unsqueeze(1).broadcast_to([P, NS[l], D])).then_inc(zeroed[l], 16)

            def load(slot, rounds, src, cols, rows=P):
                at_least(sp, stg_split[slot], *rounds)
                sp.dma_start(stg[0:rows, slot, 0:cols].rearrange("p (c n) -> p c n", n=src.shape[-1]), src)\
                    .then_inc(stg_loaded[slot], 16)

            def load_layer(l, r0):
                g = a[f"sgu{l}"].rearrange("(c p) n -> p c n", c=C)
                for n in range(4):
                    load(n, (r0, 0), g[:, n // 2:n // 2 + 1, (n % 2) * (SG // 2):(n % 2 + 1) * (SG // 2)], SG // 2)
                d = a[f"sdn{l}"][0:SFULL * P, :].rearrange("(c p) n -> p c n", p=P)
                load(0, (r0, 1), d[:, 0:2, :], 2 * D)
                load(1, (r0, 1), d[:, 2:4, :], 2 * D)
                load(2, (r0, 1), d[:, 4:5, :], D)
                load(3, (r0, 1), a[f"sdn{l}"][SFULL * P:, :].unsqueeze(1), D, SREM)

                def two_experts(base, s):
                    for k in range(2):
                        e = base * 2 + 2 * s + k if isinstance(base, int) else bass.ds(base * 2 + (2 * s + k), 1)
                        ge = a[f"gu{l}"][e] if isinstance(base, int) else a[f"gu{l}"][e, :, :].rearrange("o h n -> (o h) n")
                        de = a[f"dn{l}"][e] if isinstance(base, int) else a[f"dn{l}"][e, :, :].rearrange("o h n -> (o h) n")
                        load(2 * k, (base, r0 + 2 + s), ge.rearrange("(c p) n -> p c n", c=C), 2 * EG)
                        load(2 * k + 1, (base, r0 + 2 + s), de.rearrange("(c p) n -> p c n", c=2), 2 * D, EC)
                steps(sp, E[l] // 2, 1, 0, 0, two_experts)

            if stage >= 3:
                load_layer(0, 0)
                ffn_dma(sp, 0)
            if stage >= 6:
                load_layer(1, 2 + E[0] // 2)
                ffn_dma(sp, 1)
                for t in range(NT):
                    at_least(sp, c_used[1], 0, t + 1)
                    sp.dma_start(out.rearrange("(t p) d -> t p d", p=P)[t], x_sb[:, t, :]).then_inc(out_done, 16)
                sp.wait_ge(out_done, 16 * NT)
            else:
                sp.wait_ge(phase, 3 * {0: 1, 1: 2, 2: 3, 3: 4, 4: 6, 5: 7}[stage])
                sp.dma_start(out.rearrange("(t p) d -> p t d", p=P), x_sb[:, :, :]).then_inc(out_done, 16)
                sp.wait_ge(out_done, 16)

        def split_on_pool(pl, slot, seen, cols, hi, lo, rows=P):
            pl.wait_ge(stg_loaded[slot], seen)
            w = stg[0:rows, slot, 0:cols]
            s = swb[0:rows, 0:1].broadcast_to([rows, cols])
            nc.gpsimd.tensor_tensor(hi, w, s, ALU.mult)
            nc.gpsimd.tensor_tensor(w, w, s, ALU.mult)
            pl.drain()
            return nc.gpsimd.tensor_tensor(lo, w, hi, ALU.subtract).then_inc(stg_split[slot], 1)

        def split_layer(pl, l, r0):
            if l == 1:
                pl.wait_ge(shared_used, 1)
            for n in range(4):
                cols = slice((n % 2) * (SG // 2), (n % 2 + 1) * (SG // 2))
                split_on_pool(pl, n, 16 * (r0 + 1), SG // 2, sgu[:, 0, n // 2, cols], sgu[:, 1, n // 2, cols])
            for n in range(2):
                split_on_pool(pl, n, 16 * (r0 + 2), 2 * D, sdn[:, 0, 2 * n:2 * n + 2, :].rearrange("p c n -> p (c n)"),
                              sdn[:, 1, 2 * n:2 * n + 2, :].rearrange("p c n -> p (c n)"))
            split_on_pool(pl, 2, 16 * (r0 + 2), D, sdn[:, 0, 4, :], sdn[:, 1, 4, :])
            split_on_pool(pl, 3, 16 * (r0 + 2), D, sdn[0:SREM, 0, 5, :], sdn[0:SREM, 1, 5, :], SREM)
            pl.drain().then_inc(shared_ready[l], 1)

            if l == 1:
                pl.wait_ge(experts_used, 1)
            for e in range(E[l]):
                k, seen = e % 2, 16 * (r0 + 3 + e // 2)
                split_on_pool(pl, 2 * k, seen, 2 * EG, GU[l][:, e, 0].rearrange("p c n -> p (c n)"),
                              GU[l][:, e, 1].rearrange("p c n -> p (c n)"))
                split_on_pool(pl, 2 * k + 1, seen, 2 * D, DN[l][:, e, 0].rearrange("p c n -> p (c n)"),
                              DN[l][:, e, 1].rearrange("p c n -> p (c n)"), EC)
            pl.drain().then_inc(experts_ready[l], 1)

        @block.gpsimd
        def _(pl):
            nc.gpsimd.memset(zero[:, :], 0.0).then_inc(const_ready, 1)
            nc.gpsimd.memset(swb[:, :], SW)
            nc.gpsimd.memset(mhalf[:, :], -0.5)
            nc.gpsimd.memset(idf[:, :], 0.0)
            nc.gpsimd.memset(ones_h[:, :], 1.0)
            nc.gpsimd.memset(headmask[:, :], 1.0)
            nc.gpsimd.memset(lower[:, :, :], 1.0)
            nc.gpsimd.memset(selm[:, :, :], 0.0)
            nc.gpsimd.iota(texp[:, :], pattern=[[1, max(NS)]], base=0, channel_multiplier=0)
            pl.drain()
            nc.gpsimd.affine_select(out=idf[:, :], in_=idf[:, :], compare_op=ALU.not_equal, fill=1.0, base=0,
                                    pattern=[[-1, P]], channel_multiplier=1)
            nc.gpsimd.affine_select(out=tri[:, :], in_=ones_h[:, :], compare_op=ALU.is_gt, fill=0.0, base=0,
                                    pattern=[[1, P]], channel_multiplier=-1)
            hm = headmask[:, :].rearrange("p (b d) -> p b d", d=HD)
            nc.gpsimd.affine_select(out=hm, in_=hm, compare_op=ALU.is_ge, fill=0.0, base=0,
                                    pattern=[[-HD, P // HD], [0, HD]], channel_multiplier=1)
            nc.gpsimd.affine_select(out=lower[:, :, :], in_=lower[:, :, :], compare_op=ALU.is_gt, fill=0.0, base=0,
                                    pattern=[[1, 16], [-1, 16]], channel_multiplier=0)
            nc.gpsimd.tensor_copy(tileno[:, :], texp[:, :])
            for e in range(16):
                nc.gpsimd.memset(order[:, e:e + 1], float(16 - e))
            pl.drain()
            nc.gpsimd.affine_select(out=hm, in_=hm, compare_op=ALU.is_ge, fill=0.0, base=HD - 1,
                                    pattern=[[HD, P // HD], [0, HD]], channel_multiplier=-1)
            nc.gpsimd.tensor_copy(idh[:, :], idf[:, :])
            pl.drain().then_inc(const_ready, 1)
            for n in range(1 if stage < 2 else 2 if stage < 4 else 3 if stage < 5 else 4):
                if n == 1 and stage >= 3:
                    split_layer(pl, 0, 0)
                if n == 2:
                    ffn_pool(pl, 0)
                if n == 3 and stage >= 6:
                    split_layer(pl, 1, 2 + E[0] // 2)
                pl.wait_ge(stats_ready, n + 1)
                nc.gpsimd.tensor_tensor(rstd[:, :], ve[:, :], mhalf[:, :], ALU.pow).then_inc(rstd_ready, 1)
            if stage == 3:
                ffn_pool(pl, 0)
            if stage >= 6:
                ffn_pool(pl, 1)

        @block.scalar
        def _(act):
            act.wait_ge(ld_ctx, 16)
            nc.scalar.activation(ctxT[:, 0].rearrange("p c n -> p (c n)"), ctxf, ACT.Copy).then_inc(hi_done, 1)
            act.wait_ge(ld_w0, 16)
            nc.scalar.activation(wa0[:, 0].rearrange("p c n -> p (c n)"), w0f, ACT.Copy, scale=SW).then_inc(hi_done, 1)
            act.wait_ge(ld_w1, 16)
            nc.scalar.activation(wa1[:, 0].rearrange("p c n -> p (c n)"), w1f, ACT.Copy, scale=SW).then_inc(hi_done, 1)
            act.wait_ge(ld_rw, 32)
            for l in range(2):
                nc.scalar.activation(rw[l][:, 0].rearrange("p c n -> p (c n)"), rwf[l], ACT.Copy, scale=SW).then_inc(hi_done, 1)
            act.wait_ge(ld_small, 112)
            nc.scalar.activation(tg[:, :], g4[:, :], ACT.Tanh).then_inc(tg_ready, 1)
            for t in range(KT + 1):
                u = t % 2
                if t < KT:
                    act.wait_ge(kv_ps, t + 1)
                    if t >= 2:
                        act.wait_ge(sum_ps, t - 1)
                    nc.scalar.activation(wk1[:, 2 * u, 0:D], PS[:, u, 0:D], ACT.Exp, scale=1 / SW)
                    nc.scalar.activation(wk1[:, 2 * u, D:2 * D], PS[:, u, 0:D], ACT.Relu, scale=1 / SW)
                    nc.scalar.activation(wkh[:, 2 * u, 0:D], PS[:, u, D:2 * D], ACT.Copy, scale=1 / SW).then_inc(kv_parts, 1)
                    act.wait_ge(kv_k, t + 1)
                    nc.scalar.activation(wkh[:, 2 * u + 1, 0:D], wk1[:, 2 * u + 1, 0:D], ACT.Copy).then_inc(kv_kh, 1)
                for b in (2 * t - 2, 2 * t - 1) if t >= 1 else ():
                    act.wait_ge(sum_f, b + 1)
                    nc.scalar.activation(KV[:, 0, b].rearrange("p m k e -> p (m k e)"), la_t[b % 2],
                                         ACT.Copy).then_inc(sum_hi, 1)
            meet(act, 1)
            if stage >= 1:
                act.wait_ge(nm_ready, 1)

                def normalise(base, s):
                    at_least(act, a_xT, base, s - 1)
                    for i in range(2):
                        if isinstance(base, int):
                            t = 2 * (base + s) + i
                            xt, r, m = x_sb[:, t, :], rstd[:, t:t + 1], nmr[:, t:t + 1]
                        else:
                            t = bass.ds(base * 2 + (2 * s + i), 1)
                            xt, r, m = x_sb[:, t, :].rearrange("p o d -> p (o d)"), rstd[:, t], nmr[:, t]
                        last = nc.scalar.activation(xnf[:, 2 * (s % 2) + i, :], xt, ACT.Identity, bias=m, scale=r)
                    last.then_inc(a_xn, 1)

                def high_x(base, s):
                    at_least(act, a_xT, base, s + 1)
                    nc.scalar.activation(la_x[s % 2][0], PS[:, 0, :], ACT.Copy).then_inc(a_xh, 1)

                def batch(base, s):
                    if inside(base, s, 0, NB - 1):
                        high_x(base, s + 1)
                    if inside(base, s, 0, NB - 2):
                        normalise(base, s + 2)
                    if inside(base, s, 2, NB + 2):
                        at_least(act, a_ogT, base, s - 1)
                        at_least(act, a_out, base, s - 2)
                        nc.scalar.activation(la_oh, PS[:, 5, :], ACT.Copy).then_inc(a_ogh, 1)
                    if inside(base, s, 0, NB):
                        at_least(act, a_qg, base, s + 1)
                        at_least(act, a_phi, base, s)
                        nc.scalar.activation(la_e, PS[:, 1, :], ACT.Exp, scale=1 / SW)
                        nc.scalar.activation(la_r, PS[:, 1, :], ACT.Relu, scale=1 / SW)
                        at_least(act, a_og, base, s - 1)
                        nc.scalar.activation(la_t[s % 2], PS[:, 2, :], ACT.Tanh, scale=0.5 / SW).then_inc(a_act, 1)
                        at_least(act, a_phi, base, s + 1)
                        at_least(act, a_nd, base, s)
                        nc.scalar.activation(la_ph, la_phi, ACT.Copy).then_inc(a_phih, 1)
                normalise(0, 0)
                normalise(0, 1)
                high_x(0, 0)
                steps(act, NB + 2, 2, 3, NB - 1, batch)
                meet(act, 2)
            if stage >= 2:
                route_act(act, 0)
            if stage >= 3:
                ffn_act(act, 0)
            if stage >= 4:
                attn1_act(act)
            if stage >= 5:
                route_act(act, 1)
            if stage >= 6:
                ffn_act(act, 1)

        @block.vector
        def _(dve):
            nc.vector.memset(z_eps[:, :], Z_EPS)
            dve.wait_ge(hi_done, 1)
            nc.vector.tensor_tensor(ctxT[:, 1].rearrange("p c n -> p (c n)"), ctxf,
                                    ctxT[:, 0].rearrange("p c n -> p (c n)"), ALU.subtract).then_inc(lo_done, 1)
            for n, (w, f) in enumerate(((wa0, w0f), (wa1, w1f), (rw[0], rwf[0]), (rw[1], rwf[1]))):
                dve.wait_ge(hi_done, n + 2)
                nc.vector.scalar_tensor_tensor(w[:, 1].rearrange("p c n -> p (c n)"), f, SW,
                                               w[:, 0].rearrange("p c n -> p (c n)"), ALU.mult, ALU.subtract)\
                    .then_inc(lo_done, 1)
            dve.wait_ge(tg_ready, 1)
            nc.vector.tensor_scalar(tgw[:, :], tg[:, :], 1 / SW, None, ALU.mult)
            nc.vector.tensor_scalar(bg[:, :], bg[:, :], SW, None, ALU.mult)
            dve.drain()
            nc.vector.tensor_copy(bgh[:, 0, :], bg[:, :])
            dve.drain()
            nc.vector.tensor_tensor(bgh[:, 1, :], bg[:, :], bgh[:, 0, :], ALU.subtract)
            nc.vector.tensor_scalar(bp[:, :], bp[:, :], tg[:, 1:2], None, ALU.mult)
            dve.drain()
            nc.vector.tensor_scalar(tg[:, 0:1], tgw[:, 0:1], 0.5, None, ALU.mult).then_inc(tgw_ready, 1)
            dve.wait_ge(const_ready, 2)

            def keys_halves(t):
                u = t % 2
                dve.wait_ge(kv_parts, t + 1)
                nc.vector.scalar_tensor_tensor(wk1[:, 2 * u + 1, 0:D], wk1[:, 2 * u, 0:D], 1.0, wk1[:, 2 * u, D:2 * D],
                                               ALU.min, ALU.add).then_inc(kv_k, 1)
                nc.vector.scalar_tensor_tensor(wkh[:, 2 * u, D:2 * D], PS[:, u, D:2 * D], 1 / SW, wkh[:, 2 * u, 0:D],
                                               ALU.mult, ALU.subtract)
                dve.wait_ge(kv_kh, t + 1)
                nc.vector.tensor_tensor(wkh[:, 2 * u + 1, D:2 * D], wk1[:, 2 * u + 1, 0:D], wkh[:, 2 * u + 1, 0:D],
                                        ALU.subtract).then_inc(kv_kl, 1)

            def sums(t):
                dve.wait_ge(sum_ps, t + 1)
                for b in (2 * t, 2 * t + 1):
                    f = la_t[b % 2].rearrange("p (k e) -> p k e", e=P)
                    nc.vector.tensor_tensor(f, PS[:, 2 + 2 * (t % 2) + b % 2, :].rearrange("p (k e) -> p k e", e=P),
                                            headmask[:, :].unsqueeze(1).broadcast_to([P, 4, P]), ALU.mult).then_inc(sum_f, 1)
                    dve.wait_ge(sum_hi, b + 1)
                    nc.vector.tensor_tensor(KV[:, 1, b].rearrange("p m k e -> p (m k e)"), la_t[b % 2],
                                            KV[:, 0, b].rearrange("p m k e -> p (m k e)"), ALU.subtract)

            for t in range(KT):
                keys_halves(t)
                dve.wait_ge(ld_x, 16)
                stats(*range(NT // KT * t, NT // KT * (t + 1)))
                if t >= 1:
                    sums(t - 1)
            sums(KT - 1)
            stats_end(0)
            meet(dve, 1)
            if stage >= 1:
                dve.wait_ge(rstd_ready, 1)
                nc.vector.scalar_tensor_tensor(nmr[:, :], mv[:, :, 0], -1.0, rstd[:, :], ALU.mult, ALU.mult)\
                    .then_inc(nm_ready, 1)

                def low_x(base, s):
                    at_least(dve, a_xh, base, s + 1)
                    nc.vector.tensor_tensor(la_x[s % 2][1], PS[:, 0, :], la_x[s % 2][0], ALU.subtract).then_inc(a_xl, 1)

                def batch(base, s):
                    if inside(base, s, 0, NB - 1):
                        low_x(base, s + 1)
                    if inside(base, s, 1, NB + 1):
                        at_least(dve, a_nd, base, s)
                        z = la_z.rearrange("p i h -> p (i h)")
                        nc.vector.tensor_scalar(z, PS[:, 4, 0:2 * HEADS], Z_EPS, None, ALU.add)
                        dve.drain()
                        nc.vector.reciprocal(z, z)
                        dve.drain()
                        nc.vector.tensor_tensor(la_att.rearrange("p (h d) -> p h d", d=HD),
                                                PS[:, 3, :].rearrange("p (h d) -> p h d", d=HD), bc(z, HD), ALU.mult)
                        dve.drain()
                        at_least(dve, a_ogT, base, s - 1)
                        nc.vector.scalar_tensor_tensor(la_og, la_t[(s - 1) % 2], 1.0, la_att, ALU.add, ALU.mult)\
                            .then_inc(a_og, 1)
                    if inside(base, s, 2, NB + 2):
                        at_least(dve, a_ogh, base, s - 1)
                        nc.vector.tensor_tensor(la_ol, PS[:, 5, :], la_oh, ALU.subtract).then_inc(a_ogl, 1)
                    if inside(base, s, 0, NB):
                        at_least(dve, a_act, base, s + 1)
                        at_least(dve, a_phih, base, s)
                        nc.vector.scalar_tensor_tensor(la_phi, la_e, 1.0, la_r, ALU.min, ALU.add).then_inc(a_phi, 1)
                        at_least(dve, a_phih, base, s + 1)
                        at_least(dve, a_nd, base, s)
                        nc.vector.tensor_tensor(la_pl, la_phi, la_ph, ALU.subtract).then_inc(a_phil, 1)
                    if inside(base, s, 2, NB + 2):
                        at_least(dve, a_out, base, s - 1)
                        t = 2 * (s - 2)
                        xt = x_sb[:, t:t + 2, :].rearrange("p t d -> p (t d)")
                        nc.vector.scalar_tensor_tensor(xt, PS[:, 6, :], tg[:, 0:1], xt, ALU.mult, ALU.add).then_inc(a_x, 1)
                        stats(t, t + 1)
                low_x(0, 0)
                steps(dve, NB + 2, 2, 3, NB - 1, batch)
                stats_end(1)
                meet(dve, 2)
            if stage >= 2:
                route_dve(dve, 0)
            if stage >= 3:
                ffn_dve(dve, 0)
            if stage >= 4:
                attn1_dve(dve)
            if stage >= 5:
                route_dve(dve, 1)
            if stage >= 6:
                ffn_dve(dve, 1)

        @block.tensor
        def _(pe):
            pe.wait_ge(lo_done, 2)
            pe.wait_ge(const_ready, 2)

            def keys_values(t):
                last = mm3(PS[:, t % 2, :], lambda i, c: ctxT[:, i, c, t * P:(t + 1) * P],
                           lambda j, c: wa0[:, j, c, 2 * D:4 * D])
                last.then_inc(kv_ps, 1)
            keys_values(0)
            for t in range(KT):
                u = t % 2
                if t + 1 < KT:
                    if t >= 1:
                        pe.wait_ge(kv_kl, t)
                    keys_values(t + 1)
                pe.wait_ge(kv_kl, t + 1)
                if t >= 2:
                    pe.wait_ge(sum_f, 2 * (t - 1))
                for b in (2 * t, 2 * t + 1):
                    r = slice(SB_ * (b % 2), SB_ * (b % 2 + 1))
                    for m in range(C):
                        km = [wkh[r, 2 * u + 1, i * D + m * P:i * D + (m + 1) * P] for i in range(2)]
                        vm = [wkh[r, 2 * u, i * D + m * P:i * D + (m + 1) * P] for i in range(2)]
                        bank = PS[:, 2 + 2 * u + b % 2, m * 2 * P:(m + 1) * 2 * P]
                        for n, (i, j) in enumerate(HL):
                            nc.tensor.matmul(bank[:, 0:P], km[i], vm[j], start=(n == 0), stop=(n == 2))
                        for i in range(2):
                            last = nc.tensor.matmul(bank[:, P:2 * P], km[i], ones_h[r, :], start=(i == 0), stop=(i == 1))
                last.then_inc(sum_ps, 1)
            meet(pe, 1)
            if stage >= 1:
                def tokens(base, s):
                    at_least(pe, a_xn, base, s + 1)
                    at_least(pe, a_xl, base, s)
                    for i in range(2):
                        for c in range(C):
                            last = nc.tensor.transpose(PS[:, 0, c * TB + i * P:c * TB + (i + 1) * P],
                                                       xnf[:, 2 * (s % 2) + i, c * P:(c + 1) * P], idf[:, :])
                    last.then_inc(a_xT, 1)

                def summary(base, s, i, m, k):
                    b = base + s if isinstance(base, int) else bass.ds(base + s, 1)
                    w = KV[:, i, b, m, k, :]
                    if not isinstance(base, int):
                        w = w.rearrange("p o e -> p (o e)")
                    return w[:, ::HD] if k else w

                def batch(base, s):
                    if inside(base, s, 0, NB - 1):
                        tokens(base, s + 1)
                    if inside(base, s, 1, NB + 1):
                        at_least(pe, a_phil, base, s)
                        at_least(pe, a_og, base, s - 1)
                        for k in range(2):
                            for i in range(2):
                                for m in range(C):
                                    n_ = P // HD if k else P
                                    o_ = PS[:, 3 + k, (i * C + m) * n_:(i * C + m + 1) * n_]
                                    for n, (h, j) in enumerate(HL):
                                        last = nc.tensor.matmul(o_, (la_ph, la_pl)[h][:, m * TB + i * P:m * TB + (i + 1) * P],
                                                                summary(base, s - 1, j, m, k),
                                                                start=(n == 0), stop=(n == 2))
                        last.then_inc(a_nd, 1)
                    if inside(base, s, 0, NB):
                        at_least(pe, a_xl, base, s + 1)
                        at_least(pe, a_act, base, s)
                        for m in range(C):
                            mm3(PS[:, 1, m * TB:(m + 1) * TB], lambda i, c: wa0[:, i, c, m * P:(m + 1) * P],
                                lambda j, c: la_x[s % 2][j][:, c * TB:(c + 1) * TB])
                        for i in range(2):
                            o_ = PS[:, 2, i * D:(i + 1) * D]
                            mm3(o_, lambda h, c: la_x[s % 2][h][:, c * TB + i * P:c * TB + (i + 1) * P],
                                lambda h, c: wa0[:, h, c, D:2 * D], more=True)
                            for h in range(2):
                                last = nc.tensor.matmul(o_, ones_h[0:1, :], bgh[0:1, h, :], start=False, stop=(h == 1))
                        last.then_inc(a_qg, 1)
                    if inside(base, s, 2, NB + 2):
                        at_least(pe, a_ogl, base, s - 1)
                        at_least(pe, a_x, base, s - 2)
                        for i in range(2):
                            last = mm3(PS[:, 6, i * D:(i + 1) * D],
                                       lambda h, c: (la_oh, la_ol)[h][:, c * TB + i * P:c * TB + (i + 1) * P],
                                       lambda h, c: wa0[:, h, c, 4 * D:5 * D])
                        last.then_inc(a_out, 1)
                    if inside(base, s, 1, NB + 1):
                        at_least(pe, a_og, base, s)
                        at_least(pe, a_ogl, base, s - 1)
                        for i in range(2):
                            for c in range(C):
                                last = nc.tensor.transpose(PS[:, 5, c * TB + i * P:c * TB + (i + 1) * P],
                                                           la_og[:, i * D + c * P:i * D + (c + 1) * P], idf[:, :])
                        last.then_inc(a_ogT, 1)
                tokens(0, 0)
                steps(pe, NB + 2, 2, 3, NB - 1, batch)
                meet(pe, 2)
            if stage >= 2:
                route_pe(pe, 0)
            if stage >= 3:
                ffn_pe(pe, 0)
            if stage >= 4:
                attn1_pe(pe)
            if stage >= 5:
                route_pe(pe, 1)
            if stage >= 6:
                ffn_pe(pe, 1)


_INS = ["x", "ctxT", "wa0", "wa1", "rw0", "rw1", "gu0", "gu1", "dn0", "dn1", "sgu0", "sgu1", "sdn0", "sdn1",
        "g_xattn", "g_ffn", "bq", "bk", "bp", "bvT", "bg"]


def laid_out(inputs):
    import numpy as np
    v = {k: np.asarray(a) for k, a in inputs.items()}
    n = {}
    n["x"] = v["x"].reshape(-1, v["x"].shape[-1])
    n["ctxT"] = v["ctx_2048"].reshape(-1, v["ctx_2048"].shape[-1]).T
    n["wa0"] = np.concatenate([v["L0_xattn_Wq"].T, v["L0_xattn_Wg"].T, v["L0_xattn_Wkv"].T, v["L0_xattn_Wo"].T], 1)
    n["wa1"] = np.concatenate([v["L1_xattn_Wq"], v["L1_xattn_Wkv"], v["L1_xattn_Wp"]], 1)
    n["rw0"] = np.concatenate([v["L0_ffn_router_w"].T, v["L0_ffn_shared_gate_w"][:, None]], 1)
    n["rw1"] = np.concatenate([v["L1_ffn_router_w"].T, v["L1_ffn_se_gate_w"].T], 1)
    n["gu0"] = np.concatenate([v["L0_ffn_w_gate"], v["L0_ffn_w_up"]], 2)
    n["dn0"] = v["L0_ffn_w_down"]
    n["gu1"] = np.concatenate([v["L1_ffn_gate_w"].transpose(0, 2, 1), v["L1_ffn_up_w"].transpose(0, 2, 1)], 2)
    n["dn1"] = v["L1_ffn_down_w"].transpose(0, 2, 1)
    for l, (g, u, d) in enumerate(((v["L0_ffn_sw_gate"], v["L0_ffn_sw_up"], v["L0_ffn_sw_down"]),
                                   (v["L1_ffn_shared_gate_w"].T, v["L1_ffn_shared_up_w"].T, v["L1_ffn_shared_down_w"].T))):
        cuts = range(0, g.shape[1], 128)
        n[f"sgu{l}"] = np.concatenate([w[:, c:c + 128] for c in cuts for w in (g, u)], 1)
        n[f"sdn{l}"] = d
    n["g_xattn"], n["g_ffn"] = v["g_xattn"], v["g_ffn"]
    n["bq"], n["bp"] = v["L1_xattn_bq"], v["L1_xattn_bp"]
    n["bk"], bv = np.split(v["L1_xattn_bkv"], 2)
    n["bvT"] = bv.reshape(2, 128).T
    n["bg"] = v["L0_xattn_bg"]
    return {k: np.ascontiguousarray(n[k]) for k in _INS}


def kernel(**inputs):
    import concourse.bacc as _bacc
    from concourse import mybir as _mybir
    from concourse.bass_utils import run_bass_kernel_spmd as _run

    nc = _bacc.Bacc("TRN2", target_bir_lowering=False, num_devices=1)
    arrays = laid_out(inputs)
    aps = {k: nc.dram_tensor(k, v.shape, _mybir.dt.from_np(v.dtype), kind="ExternalInput").ap()
           for k, v in arrays.items()}
    shape = inputs["x"].shape
    out = nc.dram_tensor("out", (shape[0] * shape[1], shape[2]), _mybir.dt.float32, kind="ExternalOutput").ap()
    gated_flamingo(nc, aps, out)
    r = _run(nc, [arrays], core_ids=[0])
    return r.results[0]["out"].reshape(shape)
```
